# Optimizing a Trainium2 kernel written in Bass

```python
import numpy as np
import jax
import jax.numpy as jnp

def _softmax(x, axis=-1):
    return jax.nn.softmax(x, axis=axis)

def _gelu(x):
    return jax.nn.gelu(x, approximate=True)

def _silu(x):
    return jax.nn.silu(x)

def _sigmoid(x):
    return jax.nn.sigmoid(x)

def _layernorm(x, axis=-1, eps=1e-05):
    m = jnp.mean(x, axis=axis, keepdims=True)
    v = jnp.var(x, axis=axis, keepdims=True)
    return (x - m) / jnp.sqrt(v + eps)

def _scatter_add(tgt, idx, src, axis=0):
    return tgt.at[idx].add(src)

def _segment_sum(src, seg, n):
    return jax.ops.segment_sum(src, seg, n)
kernel_name = 'mk_early_fusion_d1_tok_img1024_r4_10bf60'

def setup_inputs(seed: int=0):
    np.random.seed(seed)
    _w = jnp.asarray

    def _rec_inputs():
        import jax
        import jax.numpy as jnp
        _rk = jax.random.key(seed)
        x = -0.00150118 + 0.499729 * jax.random.normal(jax.random.fold_in(_rk, 1), (32, 256, 64, 2), jnp.float32)
        txt = 0.00326275 + 2.8086 * jax.random.normal(jax.random.fold_in(_rk, 2), (32, 77, 256), jnp.float32)
        return (x, txt)
    x, txt = _rec_inputs()

    def _L0_tok_setup():
        import jax, jax.numpy as jnp
        import numpy as np
        import math
        H = 256
        N = 64
        CH = 1
        SEQ_L = 256
        key = jax.random.key(seed)
        k1, k2, k3, k4 = jax.random.split(key, 4)
        log_dt = jax.random.uniform(k1, (H,), dtype=jnp.float32, minval=math.log(0.001), maxval=math.log(0.1))
        inv_A_real = jnp.log(0.5 * jnp.ones((H, N), jnp.float32)) + 0.1 * jax.random.normal(k2, (H, N), dtype=jnp.float32)
        A_imag = jnp.broadcast_to(math.pi * jnp.arange(N, dtype=jnp.float32), (H, N)).copy()
        B_ri = jax.random.normal(k3, (H, N, 2), dtype=jnp.float32) * 0.5
        C_ri = jax.random.normal(k4, (CH, H, N, 2), dtype=jnp.float32) * 0.5
        return {'log_dt': log_dt, 'inv_A_real': inv_A_real, 'A_imag': A_imag, 'B_ri': B_ri, 'C_ri': C_ri, 'L': SEQ_L}
    _L0_tok_all = _L0_tok_setup()
    _L0_tok_in = {k: v for k, v in _L0_tok_all.items() if k in ('log_dt', 'inv_A_real', 'A_imag', 'B_ri')}
    del _L0_tok_all

    def _L0_attn_setup():
        import jax, jax.numpy as jnp
        import numpy as np
        N_HEAD = 16
        MASK_PENALTY = 10000.0

        def _split_heads(t, n_head):
            B, S, D = t.shape
            return t.reshape(B, S, n_head, D // n_head).transpose(0, 2, 1, 3)
        key = jax.random.key(seed)
        k1, k2, k3 = jax.random.split(key, 3)
        B, S, D = (2, 512, 256)
        x = jax.random.normal(k1, (B, S, D), dtype=jnp.float32)
        w_attn = jax.random.normal(k2, (D, 3 * D), dtype=jnp.float32) * 0.02
        b_attn = jnp.zeros((3 * D,), dtype=jnp.float32)
        w_proj = jax.random.normal(k3, (D, D), dtype=jnp.float32) * 0.02
        b_proj = jnp.zeros((D,), dtype=jnp.float32)
        return {'x': x, 'w_attn': w_attn, 'b_attn': b_attn, 'w_proj': w_proj, 'b_proj': b_proj}
    _L0_attn_all = _L0_attn_setup()
    _L0_attn_in = {k: v for k, v in _L0_attn_all.items() if k in ('w_attn', 'b_attn', 'w_proj', 'b_proj')}
    del _L0_attn_all

    def _L0_ffn_setup():
        import jax, jax.numpy as jnp
        import numpy as np
        B, S, D, H, E = (64, 256, 256, 64, 8)
        EPS = 1e-05
        key = jax.random.key(seed)
        ks = jax.random.split(key, 8)
        x = jax.random.normal(ks[0], (B, S, D), jnp.float32)
        return {'x': x, 'ln_g': jnp.ones((D,), jnp.float32), 'ln_b': jnp.zeros((D,), jnp.float32), 'bn_g': jnp.ones((D,), jnp.float32), 'bn_b': jnp.zeros((D,), jnp.float32), 'bn_mean': jax.random.normal(ks[1], (D,), jnp.float32) * 0.01, 'bn_var': jnp.ones((D,), jnp.float32), 'Wr': jax.random.normal(ks[2], (D, E), jnp.float32) * 0.02, 'br': jnp.zeros((E,), jnp.float32), 'W_down': jax.random.normal(ks[3], (E, D, H), jnp.float32) * 0.02, 'b_down': jnp.zeros((E, H), jnp.float32), 'W_up': jax.random.normal(ks[4], (E, H, D), jnp.float32) * 0.02, 'b_up': jnp.zeros((E, D), jnp.float32)}
    _L0_ffn_all = _L0_ffn_setup()
    _L0_ffn_in = {k: v for k, v in _L0_ffn_all.items() if k in ('ln_g', 'ln_b', 'bn_g', 'bn_b', 'bn_mean', 'bn_var', 'Wr', 'br', 'W_down', 'b_down', 'W_up', 'b_up')}
    del _L0_ffn_all
    return {'x': x, 'txt': txt, 'L0_tok_log_dt': _L0_tok_in['log_dt'], 'L0_tok_inv_A_real': _L0_tok_in['inv_A_real'], 'L0_tok_A_imag': _L0_tok_in['A_imag'], 'L0_tok_B_ri': _L0_tok_in['B_ri'], 'L0_attn_w_attn': _L0_attn_in['w_attn'], 'L0_attn_b_attn': _L0_attn_in['b_attn'], 'L0_attn_w_proj': _L0_attn_in['w_proj'], 'L0_attn_b_proj': _L0_attn_in['b_proj'], 'L0_ffn_ln_g': _L0_ffn_in['ln_g'], 'L0_ffn_ln_b': _L0_ffn_in['ln_b'], 'L0_ffn_bn_g': _L0_ffn_in['bn_g'], 'L0_ffn_bn_b': _L0_ffn_in['bn_b'], 'L0_ffn_bn_mean': _L0_ffn_in['bn_mean'], 'L0_ffn_bn_var': _L0_ffn_in['bn_var'], 'L0_ffn_Wr': _L0_ffn_in['Wr'], 'L0_ffn_br': _L0_ffn_in['br'], 'L0_ffn_W_down': _L0_ffn_in['W_down'], 'L0_ffn_b_down': _L0_ffn_in['b_down'], 'L0_ffn_W_up': _L0_ffn_in['W_up'], 'L0_ffn_b_up': _L0_ffn_in['b_up']}

def reference(x, txt, L0_tok_log_dt, L0_tok_inv_A_real, L0_tok_A_imag, L0_tok_B_ri, L0_attn_w_attn, L0_attn_b_attn, L0_attn_w_proj, L0_attn_b_proj, L0_ffn_ln_g, L0_ffn_ln_b, L0_ffn_bn_g, L0_ffn_bn_b, L0_ffn_bn_mean, L0_ffn_bn_var, L0_ffn_Wr, L0_ffn_br, L0_ffn_W_down, L0_ffn_b_down, L0_ffn_W_up, L0_ffn_b_up):
    import jax
    import jax.numpy as jnp

    def _L0_tok_ref(log_dt, inv_A_real, A_imag, B_ri, C_ri, L):
        import jax, jax.numpy as jnp
        import numpy as np
        import math
        H = 256
        N = 64
        CH = 1
        SEQ_L = 256
        dt = jnp.exp(log_dt)
        A = -jnp.exp(inv_A_real) + 1j * A_imag
        B = B_ri[..., 0] + 1j * B_ri[..., 1]
        C = C_ri[..., 0] + 1j * C_ri[..., 1]
        dtA = A * dt[:, None]
        dA = (1.0 + dtA / 2) / (1.0 - dtA / 2)
        C_term = C * B[None]
        log_dA = jnp.log(dA)
        V = jnp.exp(log_dA[:, :, None] * jnp.arange(L))
        K = 2.0 * jnp.einsum('chn,hnl->chl', C_term, V).real
        return K.astype(jnp.float32)

    def _L0_attn_ref(x, w_attn, b_attn, w_proj, b_proj):
        import jax, jax.numpy as jnp
        import numpy as np
        N_HEAD = 16
        MASK_PENALTY = 10000.0

        def _split_heads(t, n_head):
            B, S, D = t.shape
            return t.reshape(B, S, n_head, D // n_head).transpose(0, 2, 1, 3)
        B, S, D = x.shape
        qkv = x @ w_attn + b_attn
        q, k, v = jnp.split(qkv, 3, axis=2)
        q = _split_heads(q, N_HEAD)
        k = _split_heads(k, N_HEAD)
        v = _split_heads(v, N_HEAD)
        dh = D // N_HEAD
        w = jnp.einsum('bhqd,bhkd->bhqk', q, k) / jnp.sqrt(jnp.asarray(dh, dtype=q.dtype))
        i = jnp.arange(S)[:, None]
        j = jnp.arange(S)[None, :]
        b = (i >= j).astype(w.dtype)
        w = w * b - MASK_PENALTY * (1.0 - b)
        w = jax.nn.softmax(w, axis=-1)
        a = jnp.einsum('bhqk,bhkd->bhqd', w, v)
        a = a.transpose(0, 2, 1, 3).reshape(B, S, D)
        return a @ w_proj + b_proj

    def _L0_ffn_ref(x, ln_g, ln_b, bn_g, bn_b, bn_mean, bn_var, Wr, br, W_down, b_down, W_up, b_up):
        import jax, jax.numpy as jnp
        import numpy as np
        B, S, D, H, E = (64, 256, 256, 64, 8)
        EPS = 1e-05
        mu = jnp.mean(x, axis=-1, keepdims=True)
        var = jnp.var(x, axis=-1, keepdims=True)
        z = (x - mu) * jax.lax.rsqrt(var + EPS) * ln_g + ln_b
        z_sent = jnp.mean(z, axis=1)
        z_bn = (z_sent - bn_mean) * jax.lax.rsqrt(bn_var + EPS) * bn_g + bn_b
        probs = jax.nn.softmax(z_bn @ Wr + br, axis=-1)
        idx = jnp.argmax(probs, axis=-1)
        gate = jnp.take_along_axis(probs, idx[:, None], axis=1)[:, 0]
        h = jax.nn.relu(jnp.einsum('bsd,bdh->bsh', z, W_down[idx]) + b_down[idx][:, None, :])
        y = jnp.einsum('bsh,bhd->bsd', h, W_up[idx]) + b_up[idx][:, None, :]
        return y * gate[:, None, None]
    h = _L0_tok_ref(L0_tok_log_dt, L0_tok_inv_A_real, L0_tok_A_imag, L0_tok_B_ri, x, 256)
    h = jnp.concatenate([h, txt], axis=1)
    h = h + _L0_attn_ref(_layernorm(h, axis=-1), L0_attn_w_attn, L0_attn_b_attn, L0_attn_w_proj, L0_attn_b_proj)
    h = h + _L0_ffn_ref(_layernorm(h, axis=-1), L0_ffn_ln_g, L0_ffn_ln_b, L0_ffn_bn_g, L0_ffn_bn_b, L0_ffn_bn_mean, L0_ffn_bn_var, L0_ffn_Wr, L0_ffn_br, L0_ffn_W_down, L0_ffn_b_down, L0_ffn_W_up, L0_ffn_b_up)
    return h

_drawn_inputs = setup_inputs


def setup_inputs(seed=0):
    import zlib

    import numpy as np

    out = dict(_drawn_inputs(seed))
    spreads = {'L0_attn_b_attn': (0.0, 0.8),
     'L0_attn_b_proj': (0.0, 0.299),
     'L0_ffn_ln_g': (1.0, 0.6),
     'L0_ffn_ln_b': (0.0, 0.8),
     'L0_ffn_bn_g': (1.0, 0.6),
     'L0_ffn_bn_b': (0.0, 0.8),
     'L0_ffn_bn_var': (1.0, 0.6),
     'L0_ffn_br': (0.0, 0.8),
     'L0_ffn_b_down': (0.0, 0.8),
     'L0_ffn_b_up': (0.0, 0.8)}
    factors = {'L0_attn_w_attn': 8.0,
     'L0_attn_w_proj': 6.175,
     'L0_ffn_bn_mean': 8.0,
     'L0_ffn_Wr': 8.0,
     'L0_ffn_W_down': 8.0,
     'L0_ffn_W_up': 8.0}
    for name, (base, spread) in spreads.items():
        noise = np.random.default_rng([zlib.crc32(name.encode()), seed]).standard_normal(out[name].shape)
        drawn = base * np.exp(spread * noise) if base else spread * noise
        out[name] = jnp.asarray(drawn.astype(out[name].dtype))
    for name, factor in factors.items():
        out[name] = (out[name] * factor).astype(out[name].dtype)
    return out
```

```python
import concourse.bass as bass
from concourse import mybir
from collections import namedtuple
from contextlib import ExitStack

F32 = mybir.dt.float32
F16 = mybir.dt.float16
BF16 = mybir.dt.bfloat16
U32 = mybir.dt.uint32
ALU = mybir.AluOpType
ACT = mybir.ActivationFunctionType
AX = mybir.AxisListType

P = 128
BATCH, HK, NS, D = 32, 256, 64, 256
TXT = 77
SEQ = HK + TXT
SEQP = 3 * P
HEADS, DH = 16, 16
EXPERTS, HID = 8, 64
EPS = 1e-5
CD = D // P
MASKED = -30000.0
EULER = 2.718281828459045

HP = HK // 2
HPC = 16
CHUNKS = HP // HPC
LV = 128
SQUARINGS = 7

QT = [(0, TXT), (TXT, TXT + P), (TXT + P, SEQ)]
KT = [(0, 0), (P, P), (2 * P, 2 * P)]
W0, W1, W2 = SEQ, SEQ - P, SEQ - 2 * P


def build_tokens(nc, x, log_dt, inv_a, a_imag, b_ri, scratch):
    x_v = x.rearrange("c (h q) n r -> c h (q n r)", q=2)
    scr_v = scratch.rearrange("c (h q) l -> q c h l", q=2)
    ctx = ExitStack()
    with ctx:
        def sb(name, shape, dt=F32):
            return ctx.enter_context(nc.sbuf_tensor(name, shape, dt))

        def sem(name):
            return ctx.enter_context(nc.semaphore(name))

        ident = sb("ident1", [P, P])
        ld = sb("ld", [P, 2])
        ia = sb("ia", [P, 2, NS])
        ai = sb("ai", [P, 2, NS])
        braw = sb("braw", [P, 2, NS, 2])
        euler = sb("euler", [P, 2 * NS])
        dt = sb("dt", [P, 2])
        decay = sb("decay", [P, 2, NS])
        wr = sb("wr", [P, 2, NS])
        wi = sb("wi", [P, 2, NS])
        sq = sb("sq", [P, 2, NS])
        den = sb("den", [P, 2, NS])
        pre = sb("pre", [P, 4, 2, NS])
        bt = sb("bt", [P, 2, HP])
        zr = sb("zr", [P, SQUARINGS + 1, HP])
        zi = sb("zi", [P, SQUARINGS + 1, HP])
        nzi = sb("nzi", [P, SQUARINGS + 1, HP])
        dif = sb("dif", [P, HP])
        tot = sb("tot", [P, HP])
        xin = [sb(f"xin{q}", [P, 4, 4 * NS]) for q in range(2)]
        a = [sb(f"c{q}", [P, 2, HPC, 2, BATCH]) for q in range(2)]
        v = [sb(f"powers{q}", [P, 2, HPC, LV]) for q in range(2)]
        vtmp = sb("vtmp", [P, 2, HPC, LV // 2])
        atmp = sb("atmp", [P, 2, HPC, BATCH])
        hst = [sb(f"hst{q}", [P, HPC, LV]) for q in range(2)]
        tp = ctx.enter_context(nc.psum_tensor("tp", [P, 2, 512], F32))
        kp = [[ctx.enter_context(nc.psum_tensor(f"kp{q}{s}", [P, 4, LV], F32)) for s in range(2)] for q in range(2)]

        par_in = sem("par_in")
        ident_set = sem("ident_set")
        euler_set = sem("euler_set")
        pow_done = sem("pow_done")
        link = sem("param_link")
        pre_ready = sem("pre_ready")
        pre_t = sem("pre_transposed")
        bt_ready = sem("bt_ready")
        z_link = sem("z_link")
        z_ready = sem("z_ready")
        xin_in = [sem(f"xin_in{q}") for q in range(2)]
        ct_ready = sem("ct_ready")
        a0_ready = sem("a0_ready")
        a1_mul = sem("a1_mul")
        a1_ready = sem("a1_ready")
        v_link = sem("v_link")
        v_ready = sem("v_ready")
        k_ready = sem("k_ready")
        k_taken = sem("k_taken")
        hst_out = [sem(f"hst_out{q}") for q in range(2)]
        pool_passed = sem("pool_passed1")
        sp_passed = sem("sp_passed1")
        pe_passed = sem("pe_passed1")

        LINKS = 1 + 4 * SQUARINGS

        def chunks(eng, body):
            body(0, 0, 0)
            body(1, 0, 1)
            with eng.Fori(1, CHUNKS // 2 - 1) as m:
                body(2 * m, m, 0)
                body(2 * m + 1, m, 1)
            body(CHUNKS - 2, CHUNKS // 2 - 1, 0)
            body(CHUNKS - 1, CHUNKS // 2 - 1, 1)

        def first(k):
            return isinstance(k, int) and k < 2

        def last(k):
            return isinstance(k, int) and k == CHUNKS - 1

        with nc.Block() as block:

            @block.sync
            def _(sp):
                sp.dma_start(ld[:], log_dt.rearrange("(h q) -> h q", q=2)).then_inc(par_in, 16)
                sp.dma_start(ia[:], inv_a.rearrange("(h q) n -> h q n", q=2)).then_inc(par_in, 16)
                sp.dma_start(ai[:], a_imag.rearrange("(h q) n -> h q n", q=2)).then_inc(par_in, 16)
                sp.dma_start(braw[:], b_ri.rearrange("(h q) n r -> h q n r", q=2)).then_inc(par_in, 16)

                def body(k, m, q):
                    if not first(k):
                        sp.wait_ge(ct_ready, k - 1)
                        sp.sem_inc(sp_passed, 1)
                    for t in range(4):
                        sp.dma_start(xin[q][:, t, :], x_v[8 * t:8 * t + 8, bass.ds(HPC * k, HPC), :]).then_inc(xin_in[q], 16)
                    if not (isinstance(k, int) and k == 0):
                        store(k - 1, 1 - q)

                def store(k, q):
                    sp.wait_ge(k_taken, 8 * k + 8)
                    sp.sem_inc(sp_passed, 1)
                    for par in range(2):
                        for i in range(2):
                            p0 = 64 * par + 32 * i
                            sp.dma_start(scr_v[par, :, bass.ds(HPC * k, HPC), i * LV:(i + 1) * LV],
                                         hst[q][p0:p0 + 32, :, :]).then_inc(hst_out[q], 16)

                chunks(sp, body)
                store(CHUNKS - 1, 1)
                for q in range(2):
                    sp.wait_ge(hst_out[q], 64 * (CHUNKS // 2))

            @block.gpsimd
            def _(pool):
                pool.memset(ident[:], 0.0).then_inc(ident_set, 1)
                pool.memset(euler[:], EULER).then_inc(euler_set, 1)
                pool.wait_ge(ident_set, 1)
                pool.affine_select(out=ident[:], in_=ident[:], compare_op=ALU.not_equal, fill=1.0, base=0,
                                   pattern=[[-1, P]], channel_multiplier=1).then_inc(ident_set, 1)
                pool.wait_ge(euler_set, 1)
                pool.wait_ge(par_in, 64)
                pool.tensor_tensor(dt[:], euler[:, 0:2], ld[:], ALU.pow).then_inc(pow_done, 1)
                pool.tensor_tensor(decay[:].rearrange("p q n -> p (q n)"), euler[:],
                                   ia[:].rearrange("p q n -> p (q n)"), ALU.pow).then_inc(pow_done, 1)

                def body(k, m, q):
                    if isinstance(k, int) and k == 0:
                        pool.wait_ge(z_ready, 1)
                    pool.wait_ge(a0_ready, 2 * k + 2)
                    hs = bass.ds(HPC * k, HPC)

                    def zb(z):
                        return z[:, SQUARINGS, hs].unsqueeze(2).broadcast_to([P, HPC, BATCH])

                    src = a[q][:, :, :, 0, :]
                    dst = a[q][:, :, :, 1, :]
                    pool.tensor_tensor(dst[:, 0], src[:, 0], zb(zr), ALU.mult).then_inc(a1_mul, 1)
                    pool.tensor_tensor(dst[:, 1], src[:, 1], zb(zr), ALU.mult).then_inc(a1_mul, 1)
                    if not (isinstance(k, int) and k == 0):
                        pool.wait_ge(a1_ready, k)
                    pool.tensor_tensor(atmp[:, 0], src[:, 1], zb(zi), ALU.mult).then_inc(a1_mul, 1)
                    pool.tensor_tensor(atmp[:, 1], src[:, 0], zb(nzi), ALU.mult).then_inc(a1_mul, 1)
                    pool.wait_ge(a1_mul, 4 * k + 4)
                    pool.tensor_tensor(dst, dst, atmp[:], ALU.add).then_inc(a1_ready, 1)

                chunks(pool, body)

            @block.scalar
            def _(act):
                act.wait_ge(z_link, 2)
                act.copy(bt[:, :, :], tp[:, 0, 256:512].rearrange("p (r h) -> p r h", r=2)).then_inc(bt_ready, 1)

                def take_c(k, q):
                    act.wait_ge(ct_ready, k + 1)
                    if not first(k):
                        act.wait_ge(k_ready, 4 * k - 4)
                    for ri in range(2):
                        act.mul(a[q][:, ri, :, 0, :].rearrange("p h c -> p c h"),
                                tp[:, ri, :].rearrange("p (c h) -> p c h", h=HPC),
                                1.0 - 2.0 * ri).then_inc(a0_ready, 1)

                take_c(0, 0)

                def body(k, m, q):
                    if not last(k):
                        take_c(k + 1, 1 - q)
                    if not first(k):
                        act.wait_ge(hst_out[q], 64 * m)
                    for g in range(4):
                        act.wait_ge(k_ready, 4 * k + g + 1)
                        for par in range(2):
                            rows = slice(64 * par, 64 * par + 64)
                            act.copy(hst[q][rows, 4 * g:4 * g + 4, :], kp[par][g % 2][rows, :, :]).then_inc(k_taken, 1)

                chunks(act, body)

            @block.vector
            def _(dve):
                n = [0]

                def step(ins):
                    n[0] += 1
                    ins.then_inc(link, 1)

                def done():
                    dve.wait_ge(link, n[0])

                dve.wait_ge(pow_done, 2)
                dve.wait_ge(par_in, 64)
                dtb = dt[:].unsqueeze(2).broadcast_to([P, 2, NS])
                step(dve.scalar_tensor_tensor(wr[:], decay[:], -0.5, dtb, ALU.mult, ALU.mult))
                step(dve.scalar_tensor_tensor(wi[:], ai[:], 0.5, dtb, ALU.mult, ALU.mult))
                done()
                step(dve.tensor_scalar(sq[:], wr[:], -1.0, 1.0, ALU.mult, ALU.add))
                step(dve.tensor_tensor(tot[:].rearrange("p (q n) -> p q n", q=2), wi[:], wi[:], ALU.mult))
                done()
                wi2 = tot[:].rearrange("p (q n) -> p q n", q=2)
                step(dve.tensor_tensor(den[:], sq[:], sq[:], ALU.mult))
                step(dve.scalar_tensor_tensor(pre[:, 0], wr[:], 1.0, sq[:], ALU.add, ALU.mult))
                done()
                step(dve.tensor_tensor(den[:], den[:], wi2, ALU.add))
                step(dve.tensor_tensor(pre[:, 0], pre[:, 0], wi2, ALU.subtract))
                done()
                step(dve.reciprocal(den[:], den[:]))
                done()
                dve.tensor_tensor(pre[:, 0], pre[:, 0], den[:], ALU.mult).then_inc(pre_ready, 1)
                dve.scalar_tensor_tensor(pre[:, 1], wi[:], 2.0, den[:], ALU.mult, ALU.mult).then_inc(pre_ready, 1)
                dve.tensor_scalar(pre[:, 2], braw[:, :, :, 0], 2.0, None, ALU.mult).then_inc(pre_ready, 1)
                dve.tensor_scalar(pre[:, 3], braw[:, :, :, 1], 2.0, None, ALU.mult).then_inc(pre_ready, 1)
                dve.wait_ge(pre_t, 1)
                c = 0

                def zstep(ins):
                    ins.then_inc(z_link, 1)

                zstep(dve.tensor_copy(zr[:, 0, :], tp[:, 0, 0:P]))
                zstep(dve.tensor_copy(zi[:, 0, :], tp[:, 0, P:2 * P]))
                c += 2
                for k in range(SQUARINGS):
                    dve.wait_ge(z_link, c)
                    zstep(dve.tensor_tensor(dif[:], zr[:, k], zi[:, k], ALU.subtract))
                    zstep(dve.tensor_tensor(tot[:], zr[:, k], zi[:, k], ALU.add))
                    zstep(dve.scalar_tensor_tensor(zi[:, k + 1], zr[:, k], 2.0, zi[:, k], ALU.mult, ALU.mult))
                    c += 3
                    dve.wait_ge(z_link, c)
                    zstep(dve.tensor_tensor(zr[:, k + 1], dif[:], tot[:], ALU.mult))
                    c += 1
                dve.wait_ge(z_link, c)
                zstep(dve.tensor_scalar(nzi[:], zi[:], -1.0, None, ALU.mult))
                c += 1
                dve.wait_ge(z_link, c)
                dve.tensor_copy(dif[:, 0:1], dt[:, 0:1]).then_inc(z_ready, 1)

                def body(k, m, q):
                    hs = bass.ds(HPC * k, HPC)
                    base = LINKS * k
                    if isinstance(k, int) and k == 0:
                        dve.wait_ge(bt_ready, 1)
                    if not first(k):
                        dve.wait_ge(k_ready, 4 * k - 4)
                    dve.tensor_copy(v[q][:, :, :, 0:1], bt[:, :, hs].unsqueeze(3)).then_inc(v_link, 1)
                    c = 1
                    for s in range(SQUARINGS):
                        w = 1 << s

                        def zb(z):
                            return z[:, s, hs].unsqueeze(2).broadcast_to([P, HPC, w])

                        lo = v[q][:, :, :, 0:w]
                        hi = v[q][:, :, :, w:2 * w]
                        tmp = vtmp[:, :, :, 0:w]
                        dve.wait_ge(v_link, base + c)
                        dve.tensor_tensor(tmp[:, 0], lo[:, 1], zb(nzi), ALU.mult).then_inc(v_link, 1)
                        dve.tensor_tensor(tmp[:, 1], lo[:, 0], zb(zi), ALU.mult).then_inc(v_link, 1)
                        dve.tensor_tensor(hi, lo, z_both(s, hs, w), ALU.mult).then_inc(v_link, 1)
                        c += 3
                        dve.wait_ge(v_link, base + c)
                        ins = dve.tensor_tensor(hi, hi, tmp, ALU.add)
                        c += 1
                        if s == SQUARINGS - 1:
                            ins.then_inc(v_ready, 1)
                            dve.sem_inc(v_link, 1)
                        else:
                            ins.then_inc(v_link, 1)

                def z_both(s, hs, w):
                    return zr[:, s, hs].unsqueeze(1).unsqueeze(3).broadcast_to([P, 2, HPC, w])

                chunks(dve, body)

            @block.tensor
            def _(pe):
                pe.wait_ge(ident_set, 2)
                pe.wait_ge(pre_ready, 4)
                for j in range(4):
                    ins = pe.transpose(tp[:, 0, P * j:P * j + P], pre[:, j].rearrange("p q n -> p (q n)"), ident[:])
                ins.then_inc(pre_t, 1)
                pe.wait_ge(bt_ready, 1)
                pe.wait_ge(z_link, 2)

                def turn_c(k, m, q):
                    pe.wait_ge(xin_in[q], 64 * m + 64)
                    if not (isinstance(k, int) and k == 0):
                        pe.wait_ge(a0_ready, 2 * k)
                    for ri in range(2):
                        for t in range(4):
                            src = xin[q][:, t, :].rearrange("p (f r) -> p r f", r=2)[:, ri, :]
                            ins = pe.transpose(tp[:, ri, P * t:P * t + P], src, ident[:])
                    ins.then_inc(ct_ready, 1)

                turn_c(0, 0, 0)

                def body(k, m, q):
                    if not last(k):
                        turn_c(k + 1, m if q == 0 else m + 1, 1 - q)
                    pe.wait_ge(v_ready, k + 1)
                    pe.wait_ge(a1_ready, k + 1)
                    for g in range(4):
                        if not (isinstance(k, int) and k == 0 and g < 2):
                            pe.wait_ge(k_taken, 8 * k + 2 * g - 2)
                        pe.sem_inc(pe_passed, 1)
                        for h in range(4 * g, 4 * g + 4):
                            for par in range(2):
                                rows = slice(64 * par, 64 * par + 64)
                                for ri in range(2):
                                    ins = pe.matmul(kp[par][g % 2][rows, h % 4, :],
                                                    a[q][rows, ri, h, :, :].rearrange("p i c -> p (i c)"),
                                                    v[q][rows, ri, h, :], start=ri == 0, stop=ri == 1)
                        ins.then_inc(k_ready, 1)

                chunks(pe, body)


STEPS = [
    [("xt0", 1), ("xt1", 1), ("rt", -2)],
    [("q0", 1), ("k0", 1), ("q1", 1)],
    [("k1", 1), ("fd", -2), ("v01", 1)],
    [("fu01", -2), ("nm1", 0), ("fu2", -2)],
    [("v2", 1), ("ot0", -1), ("ot1", -1)],
    [("ot2", -1), ("ox0", -1), ("ox1", -1)],
    [("pr01", -1), ("pr2", -1)],
    [("nm0", 1), ("zt0", -1), ("zt1", -1)],
]
SLICES = [s for step in STEPS for s in step]
JOBS = 8
PSLOTS = 4
Batch = namedtuple("Batch", "at half par")


def batch(m, e):
    return Batch(2 * m + e, m + e // 2, e % 2)


def live(b):
    return not isinstance(b.at, int) or 0 <= b.at < BATCH


def iterations(eng, body):
    for i in range(-1, 3):
        body(0, i)
    with eng.Fori(1, BATCH // 2 - 2) as m:
        body(m, 1)
        body(m, 2)
    for i in range(BATCH - 3, BATCH + 2):
        body(0, i)


def need(eng, sem, count):
    if not isinstance(count, int) or count > 0:
        eng.wait_ge(sem, count)


def score_job(m, e, j):
    return (batch(m, e + 1), j - 3) if j >= 3 else (batch(m, e), j + 5)


def pv_group(m, e, j):
    if j % 2:
        return None
    b, g = (batch(m, e - 1), 3) if j == 0 else (batch(m, e), j // 2 - 1)
    return (b, g) if live(b) else None


def slice_before(m, e, k):
    while True:
        k -= 1
        if k < 0:
            k += len(SLICES)
            e -= 1
        if e < -1 and isinstance(m, int):
            return None
        name, d = SLICES[k]
        if live(batch(m, e + d)):
            return name, batch(m, e + d)


def build_layer(nc, scratch, txt, w_attn, b_attn, w_proj, b_proj, ln_g, ln_b, bn_g, bn_b, bn_mean, bn_var,
                w_r, b_r, w_down, b_down, w_up, b_up, out):
    ctx = ExitStack()
    with ctx:
        def sb(name, shape, dt=F32):
            return ctx.enter_context(nc.sbuf_tensor(name, shape, dt))

        def sem(name):
            return ctx.enter_context(nc.semaphore(name))

        ident = sb("ident", [P, P])
        ident16 = sb("ident16", [P, P], BF16)
        later = sb("later", [P, P], BF16)
        pick = sb("pick", [P, 8, P], BF16)
        minus_half = sb("minus_half", [P, 4])
        halves = sb("halves", [P, 8])
        wa = sb("wa", [P, CD, 3 * D])
        wp = sb("wp", [P, CD, D])
        wrt = sb("wrt", [P, CD, EXPERTS])
        bqk = sb("bqk", [P, 4])
        bv = sb("bv", [P, HEADS, DH])
        bp = sb("bp", [P, D])
        brt = sb("brt", [P, EXPERTS])
        lng = sb("lng", [P, CD])
        lnb = sb("lnb", [P, CD])
        bng = sb("bng", [P, CD])
        bnb = sb("bnb", [P, CD])
        bnm = sb("bnm", [P, CD])
        bnv = sb("bnv", [P, CD])
        bns = sb("bns", [P, CD])
        bnt = sb("bnt", [P, CD])
        h = sb("h", [P, 3, D])
        stats = sb("stats", [P, 3, 6])
        mv = sb("mv", [P, 3, 2])
        var1 = sb("var1", [P, 3])
        rstd1 = sb("rstd1", [P, 3])
        xn = sb("xn", [P, 3, D])
        xnt = sb("xnt", [P, CD, SEQ])
        qs = [sb(f"qs{q}", [P, CD, 2, SEQ], F16) for q in range(2)]
        ks = sb("ks", [P, CD, 2, SEQ], F16)
        km = [sb(f"km{q}", [P, HEADS, 2, SEQP], F16) for q in range(2)]
        v = [sb(f"v{q}", [P, 3, HEADS, 2 * DH]) for q in range(2)]
        mx = [sb(f"mx{u}", [P, 3, P]) for u in range(2)]
        nmt = [sb(f"nmt{u}", [P, SEQ], BF16) for u in range(2)]
        pr = [sb(f"pr{s}", [P, 3, W0 + W2]) for s in range(PSLOTS)]
        ot = [sb(f"ot{q}", [P, 4, SEQ]) for q in range(2)]
        rden = sb("rden", [P, HEADS])
        on = sb("on", [P, 3, D])
        ont = sb("ont", [P, CD, SEQ])
        res = sb("res", [P, 3, D])
        h2 = sb("h2", [P, 3, D])
        stats2 = sb("stats2", [P, 3, 6])
        mv2 = sb("mv2", [P, 3, 2])
        var2 = sb("var2", [P, 3])
        rstd2 = sb("rstd2", [P, 3])
        zn = sb("zn", [P, 3, D])
        zt = sb("zt", [P, CD, SEQ])
        zsum = sb("zsum", [P, CD])
        zb = sb("zb", [P, CD])
        logit = sb("logit", [P, EXPERTS])
        top = sb("top", [P, 8])
        topi = sb("topi", [P, 8], U32)
        shifted = sb("shifted", [P, EXPERTS])
        expd = sb("expd", [P, EXPERTS])
        esum = sb("esum", [P, 1])
        gate = sb("gate", [P, 1])
        wd = sb("wd", [P, CD, HID])
        wu = sb("wu", [HID + 1, D])
        bd = sb("bd", [HID, 1])
        hid = sb("hid", [HID + 1, SEQ])
        ob = sb("ob", [P, 3, D])

        st = ctx.enter_context(nc.psum_tensor("st", [P, 3, 512], F32))
        sc = ctx.enter_context(nc.psum_tensor("sc", [P, 3, 512], F32))
        otp = ctx.enter_context(nc.psum_tensor("otp", [P, 512], F32))
        db = ctx.enter_context(nc.psum_tensor("db", [P, 512], F32))

        weights_in = sem("weights_in")
        pool_set = sem("pool_set")
        dve_set = sem("dve_set")
        setup_done = sem("setup_done")
        made = {n: sem(f"made_{n}") for n, _ in SLICES}
        taken = {n: sem(f"taken_{n}") for n, _ in SLICES}
        h_in = sem("h_in")
        stats_ready = sem("stats_ready")
        mv_ready = sem("mv_ready")
        var_ready = sem("var_ready")
        rstd_ready = sem("rstd_ready")
        xn_ready = sem("xn_ready")
        qh_ready = sem("qh_ready")
        kh_ready = sem("kh_ready")
        km_ready = sem("km_ready")
        sc_ready = sem("sc_ready")
        mx_ready = sem("mx_ready")
        st_ready = sem("st_ready")
        exp_done = sem("exp_done")
        causal = sem("causal")
        pv_done = sem("pv_done")
        ot_taken = sem("ot_taken")
        rden_ready = sem("rden_ready")
        res_in = sem("res_in")
        res_ready = sem("res_ready")
        stats2_ready = sem("stats2_ready")
        mv2_ready = sem("mv2_ready")
        var2_ready = sem("var2_ready")
        rstd2_ready = sem("rstd2_ready")
        zn_ready = sem("zn_ready")
        zb_mul = sem("zb_mul")
        zb_ready = sem("zb_ready")
        top_ready = sem("top_ready")
        topi_ready = sem("topi_ready")
        shifted_ready = sem("shifted_ready")
        esum_ready = sem("esum_ready")
        gate_ready = sem("gate_ready")
        expert_in = sem("expert_in")
        stored = sem("stored")
        passed = {n: sem(f"passed_{n}") for n in ("sp", "pool", "dve", "pe")}

        NEED_POOL = 14

        with nc.Block() as block:

            @block.sync
            def _(sp):
                col = "(c p) -> p c"
                sp.dma_start(wa[:], w_attn.rearrange("(c p) n -> p c n", p=P)).then_inc(weights_in, 16)
                sp.dma_start(wp[:], w_proj.rearrange("(c p) n -> p c n", p=P)).then_inc(weights_in, 16)
                sp.dma_start(wrt[:], w_r.rearrange("(c p) n -> p c n", p=P)).then_inc(weights_in, 16)
                sp.dma_start(bqk[:], b_attn[0:2 * D].rearrange(col, p=P), allow_slow_non_contiguous=True).then_inc(weights_in, 16)
                sp.dma_start(bv[:].rearrange("p h d -> p (h d)"),
                             b_attn[2 * D:3 * D].unsqueeze(0).broadcast_to([P, D])).then_inc(weights_in, 16)
                sp.dma_start(bp[:], b_proj.unsqueeze(0).broadcast_to([P, D])).then_inc(weights_in, 16)
                sp.dma_start(brt[:], b_r.unsqueeze(0).broadcast_to([P, EXPERTS])).then_inc(weights_in, 16)
                for dst, src in ((lng, ln_g), (lnb, ln_b), (bng, bn_g), (bnb, bn_b), (bnm, bn_mean), (bnv, bn_var)):
                    sp.dma_start(dst[:], src.rearrange(col, p=P), allow_slow_non_contiguous=True).then_inc(weights_in, 16)
                sp.wait_ge(pool_set, NEED_POOL)
                sp.wait_ge(dve_set, 1)

                def load(dst, b, sm):
                    sp.dma_start(dst[:, 0:2, :], scratch[bass.ds(b.at, 1), :, :].rearrange("b (t p) l -> p (b t) l", p=P)).then_inc(sm, 16)
                    sp.dma_start(dst[0:TXT, 2:3, :], txt[bass.ds(b.at, 1), :, :].rearrange("b p l -> p b l")).then_inc(sm, 16)

                def body(m, e):
                    if e == -1:
                        load(h, batch(m, 0), h_in)
                    b = batch(m, e + 2)
                    if live(b):
                        need(sp, xn_ready, 3 * b.at)
                        sp.sem_inc(passed["sp"], 1)
                        load(h, b, h_in)
                    b = batch(m, e - 1)
                    if live(b):
                        need(sp, taken["pr2"], b.at)
                        sp.sem_inc(passed["sp"], 1)
                        load(res, b, res_in)
                    b = batch(m, e - 2)
                    if live(b):
                        sp.wait_ge(topi_ready, b.at + 1)
                        sp.sem_inc(passed["sp"], 1)
                        x = sp.value_load(topi[0:1, 0:1], min_val=0, max_val=EXPERTS - 1)
                        one = bass.ds(x, 1)
                        sp.dma_start(wd[:], w_down[one, :, :].rearrange("e (c p) f -> p (e c) f", p=P)).then_inc(expert_in, 16)
                        sp.dma_start(bd[:], b_down[one, :].rearrange("e f -> f e"), allow_slow_non_contiguous=True).then_inc(expert_in, 16)
                        sp.dma_start(wu[0:HID, :], w_up[one, :, :].rearrange("e f d -> (e f) d")).then_inc(expert_in, 16)
                        sp.dma_start(wu[HID:HID + 1, :], b_up[one, :]).then_inc(expert_in, 16)
                        sp.wait_ge(taken["fu2"], b.at + 1)
                        sp.sem_inc(passed["sp"], 1)
                        o = out[bass.ds(b.at, 1), :, :]
                        sp.dma_start(o[:, 0:HK, :].rearrange("b (t p) l -> p (b t) l", p=P), ob[:, 0:2, :]).then_inc(stored, 16)
                        sp.dma_start(o[:, HK:SEQ, :].rearrange("b p l -> p b l"), ob[0:TXT, 2:3, :]).then_inc(stored, 16)

                iterations(sp, body)
                sp.wait_ge(stored, 32 * BATCH)

            @block.gpsimd
            def _(pool):
                pool.memset(ident[:], 0.0).then_inc(pool_set, 1)
                pool.memset(ident16[:], 0.0).then_inc(pool_set, 1)
                pool.memset(later[:], 0.0).then_inc(pool_set, 1)
                pool.memset(pick[:], 1.0).then_inc(pool_set, 1)
                pool.memset(minus_half[:], -0.5).then_inc(pool_set, 1)
                pool.memset(halves[:], 1.0).then_inc(pool_set, 1)
                pool.wait_ge(pool_set, 6)
                for t in (ident, ident16):
                    pool.affine_select(out=t[:], in_=t[:], compare_op=ALU.not_equal, fill=1.0, base=0,
                                       pattern=[[-1, P]], channel_multiplier=1).then_inc(pool_set, 1)
                pool.affine_select(out=later[:], in_=later[:], compare_op=ALU.is_ge, fill=MASKED, base=0,
                                   pattern=[[-1, P]], channel_multiplier=1).then_inc(pool_set, 1)
                pool.affine_select(out=pick[:], in_=pick[:], compare_op=ALU.is_equal, fill=0.0, base=0,
                                   pattern=[[-1, 8], [0, P]], channel_multiplier=1).then_inc(pool_set, 1)
                pool.affine_select(out=halves[:], in_=halves[:], compare_op=ALU.is_ge, fill=0.0, base=0,
                                   pattern=[[-DH, 8]], channel_multiplier=1).then_inc(pool_set, 1)
                pool.wait_ge(pool_set, 11)
                pool.affine_select(out=halves[:], in_=halves[:], compare_op=ALU.is_ge, fill=0.0, base=DH - 1,
                                   pattern=[[DH, 8]], channel_multiplier=-1).then_inc(pool_set, 1)
                pool.wait_ge(dve_set, 1)
                pool.wait_ge(weights_in, 13 * 16)
                pool.tensor_scalar(bns[:], bnv[:], 1.0, EPS, ALU.mult, ALU.add).then_inc(pool_set, 1)
                pool.wait_ge(pool_set, 13)
                pool.tensor_tensor(bns[:], bns[:], minus_half[:, 0:CD], ALU.pow).then_inc(pool_set, 1)

                def power(src, scale, eps, var, rstd, b, got, mid, ready):
                    pool.wait_ge(got, 3 * b.at + 3)
                    pool.sem_inc(passed["pool"], 1)
                    pool.tensor_scalar(var[:], src[:, :, 1], scale, eps, ALU.mult, ALU.add).then_inc(mid, 1)
                    pool.wait_ge(mid, b.at + 1)
                    pool.sem_inc(passed["pool"], 1)
                    pool.tensor_tensor(rstd[:], var[:], minus_half[:, 0:3], ALU.pow).then_inc(ready, 1)

                def body(m, e):
                    now = batch(m, e)
                    for j in range(JOBS):
                        if live(now):
                            p = pr[j % PSLOTS]
                            pool.wait_ge(exp_done, 2 * (JOBS * now.at + j) + 2)
                            pool.sem_inc(passed["pool"], 1)
                            two = [[0, 2], [1, P]]
                            for ap, pat in ((p[:, 0:2, 0:P], two),
                                            (p[:, 2, :].rearrange("p (a c) -> p a c", c=W1)[:, :, 0:P], two),
                                            (p[:, 0:2, W0:W0 + W2], [[0, 2], [1, W2]])):
                                pool.affine_select(out=ap, in_=ap, compare_op=ALU.is_ge, fill=0.0, base=0,
                                                   pattern=pat, channel_multiplier=-1).then_inc(causal, 1)
                        b = batch(m, e - 1)
                        if j == 3 and live(b):
                            pool.wait_ge(res_in, 32 * b.at + 32)
                            pool.sem_inc(passed["pool"], 1)
                            pool.tensor_tensor(res[:], res[:], bp[:].unsqueeze(1).broadcast_to([P, 3, D]), ALU.add).then_inc(res_ready, 1)
                        if j == 5 and live(batch(m, e + 2)):
                            power(mv, 1.0, EPS, var1, rstd1, batch(m, e + 2), mv_ready, var_ready, rstd_ready)
                        if j == 6 and live(b):
                            power(mv2, 1.0 + EPS, EPS * EPS, var2, rstd2, b, mv2_ready, var2_ready, rstd2_ready)

                power(mv, 1.0, EPS, var1, rstd1, batch(0, 0), mv_ready, var_ready, rstd_ready)
                iterations(pool, body)

            @block.scalar
            def _(act):
                act.wait_ge(dve_set, 1)
                act.wait_ge(pool_set, NEED_POOL)

                def take(name, b):
                    if name in ("xt0", "xt1"):
                        act.wait_ge(made[name], b.at + 1)
                        act.copy(xnt[:, int(name[2]), :], db[:, 0:SEQ]).then_inc(taken[name], 1)
                    elif name in ("q0", "q1"):
                        c = int(name[1])
                        act.wait_ge(made[name], b.at + 1)
                        act.activation(qs[b.par][:, c, 0, :], db[:, 0:SEQ], ACT.Identity, bias=bqk[:, c:c + 1]).then_inc(qh_ready, 1)
                    elif name in ("k0", "k1"):
                        c = int(name[1])
                        act.wait_ge(made[name], b.at + 1)
                        need(act, km_ready, HEADS * b.at)
                        act.activation(ks[:, c, 0, :], db[:, 0:SEQ], ACT.Identity, bias=bqk[:, 2 + c:3 + c]).then_inc(kh_ready, 1)
                    elif name in ("nm0", "nm1"):
                        act.wait_ge(made[name], b.at + 1)
                        act.mul(nmt[int(name[2])][:], db[:, 0:SEQ], -1.0).then_inc(taken[name], 1)
                    elif name in ("ox0", "ox1"):
                        act.wait_ge(made[name], b.at + 1)
                        act.copy(ont[:, int(name[2]), :], db[:, 0:SEQ]).then_inc(taken[name], 1)
                    elif name in ("zt0", "zt1"):
                        c = int(name[2])
                        act.wait_ge(made[name], b.at + 1)
                        act.activation(zt[:, c, :], db[:, 0:SEQ], ACT.Identity, bias=lnb[:, c:c + 1], scale=lng[:, c:c + 1],
                                       accum_out=zsum[:, c:c + 1]).then_inc(taken[name], 1)
                    elif name == "rt":
                        act.wait_ge(shifted_ready, b.at + 1)
                        act.activation(expd[:], shifted[:], ACT.Exp, accum_out=esum[:]).then_inc(esum_ready, 1)
                    elif name == "fd":
                        act.wait_ge(made[name], b.at + 1)
                        act.activation(hid[0:HID, :], db[0:HID, 0:SEQ], ACT.Relu, bias=bd[:]).then_inc(taken[name], 1)

                def body(m, e):
                    now = batch(m, e)
                    for j in range(JOBS):
                        slices = [(n, batch(m, e + d)) for n, d in STEPS[j] if live(batch(m, e + d))]
                        if live(now):
                            p = pr[j % PSLOTS]
                            act.wait_ge(st_ready, JOBS * now.at + j + 1)
                            need(act, pv_done, 4 * now.at + j // 2 - 1)
                            act.activation(p[:, 0:2, :], st[:, 0:2, 0:W0 + W2], ACT.Exp).then_inc(exp_done, 1)
                            act.activation(p[:, 2, :], st[:, 2, 0:2 * W1], ACT.Exp).then_inc(exp_done, 1)
                        for n, b in slices:
                            take(n, b)
                        g = pv_group(m, e, j)
                        if g is not None:
                            b, g = g
                            act.wait_ge(pv_done, 4 * b.at + g + 1)
                            act.copy(ot[b.par][:, g, :], otp[:, 0:SEQ]).then_inc(ot_taken, 1)

                iterations(act, body)

            @block.vector
            def _(dve):
                for q in range(2):
                    dve.memset(km[q][:], 0.0)
                    dve.memset(v[q][:], 0.0)
                    dve.memset(mx[q][:], 0.0)
                dve.memset(hid[HID:HID + 1, :], 1.0)
                dve.memset(h[:, 2, :], 0.0)
                dve.memset(res[:, 2, :], 0.0)
                dve.memset(h2[:, 2, :], 0.0)
                dve.memset(on[:, 2, :], 0.0).then_inc(setup_done, 1)
                dve.wait_ge(setup_done, 1)
                for q in range(2):
                    dve.memset(v[q][:, :, :, DH:DH + 1], 1.0)
                dve.wait_ge(weights_in, 13 * 16)
                dve.tensor_scalar(bqk[:, 0:2], bqk[:, 0:2], 0.25, None, ALU.mult)
                dve.tensor_scalar(wa[:, :, 0:D], wa[:, :, 0:D], 0.25, None, ALU.mult).then_inc(dve_set, 1)
                dve.wait_ge(pool_set, NEED_POOL)
                dve.tensor_tensor(bns[:], bns[:], bng[:], ALU.mult).then_inc(setup_done, 1)
                dve.wait_ge(setup_done, 2)
                dve.tensor_tensor(bnt[:], bns[:], bnm[:], ALU.mult).then_inc(setup_done, 1)
                dve.wait_ge(setup_done, 3)
                dve.tensor_tensor(bnt[:], bnb[:], bnt[:], ALU.subtract)
                dve.tensor_scalar(bns[:], bns[:], 1.0 / SEQ, None, ALU.mult).then_inc(setup_done, 1)
                dve.wait_ge(setup_done, 4)

                def statistics(src, stat, mean_var, b, ready, done):
                    for t in range(3):
                        dve.bn_stats(stat[:, t, :], src[:, t, :]).then_inc(ready, 1)
                    dve.wait_ge(ready, 3 * b.at + 3)
                    dve.sem_inc(passed["dve"], 1)
                    for t in range(3):
                        dve.bn_aggr(mean_var[:, t, :], stat[:, t, :]).then_inc(done, 1)

                def normalise(dst, src, mean_var, rstd, b, got, done):
                    dve.wait_ge(got, b.at + 1)
                    dve.sem_inc(passed["dve"], 1)
                    for t in range(3):
                        dve.tensor_scalar(dst[:, t, :], src[:, t, :], mean_var[:, t, 0:1], rstd[:, t:t + 1],
                                          ALU.subtract, ALU.mult).then_inc(done, 1)

                def first_norm_stats(b):
                    dve.wait_ge(h_in, 32 * b.at + 32)
                    statistics(h, stats, mv, b, stats_ready, mv_ready)

                def take(name, b):
                    if name in ("q0", "q1"):
                        c = int(name[1])
                        dve.wait_ge(qh_ready, 2 * b.at + c + 1)
                        dve.scalar_tensor_tensor(qs[b.par][:, c, 1, :], db[:, 0:SEQ], bqk[:, c:c + 1], qs[b.par][:, c, 0, :],
                                                 ALU.add, ALU.subtract).then_inc(taken[name], 1)
                    elif name in ("k0", "k1"):
                        c = int(name[1])
                        dve.wait_ge(kh_ready, 2 * b.at + c + 1)
                        dve.scalar_tensor_tensor(ks[:, c, 1, :], db[:, 0:SEQ], bqk[:, 2 + c:3 + c], ks[:, c, 0, :],
                                                 ALU.add, ALU.subtract).then_inc(taken[name], 1)
                    elif name == "v01":
                        dve.wait_ge(made[name], b.at + 1)
                        dve.tensor_tensor(v[b.par][:, 0:2, :, 0:DH], db[:].rearrange("p (t h d) -> p t h d", t=2, d=DH),
                                          bv[:].unsqueeze(1).broadcast_to([P, 2, HEADS, DH]), ALU.add).then_inc(taken[name], 1)
                    elif name == "v2":
                        dve.wait_ge(made[name], b.at + 1)
                        dve.tensor_tensor(v[b.par][0:TXT, 2, :, 0:DH], db[0:TXT, 0:D].rearrange("p (h d) -> p h d", d=DH),
                                          bv[0:TXT], ALU.add).then_inc(taken[name], 1)
                    elif name in ("ot0", "ot1", "ot2"):
                        t = int(name[2])
                        n = TXT if t == 2 else P
                        o = db[0:n, :].rearrange("p (h d) -> p h d", d=2 * DH)
                        dve.wait_ge(made[name], b.at + 1)
                        dve.reciprocal(rden[0:n, :], o[:, :, DH]).then_inc(rden_ready, 1)
                        dve.wait_ge(rden_ready, 3 * b.at + t + 1)
                        dve.tensor_tensor(on[0:n, t, :].rearrange("p (h d) -> p h d", d=DH), o[:, :, 0:DH],
                                          rden[0:n, :].unsqueeze(2).broadcast_to([n, HEADS, DH]), ALU.mult).then_inc(taken[name], 1)
                    elif name == "pr01":
                        dve.wait_ge(res_ready, b.at + 1)
                        dve.wait_ge(made[name], b.at + 1)
                        dve.tensor_tensor(h2[:, 0:2, :], db[:].rearrange("p (t n) -> p t n", t=2), res[:, 0:2, :],
                                          ALU.add).then_inc(taken[name], 1)
                    elif name == "pr2":
                        dve.wait_ge(made[name], b.at + 1)
                        dve.tensor_tensor(h2[0:TXT, 2, :], db[0:TXT, 0:D], res[0:TXT, 2, :], ALU.add).then_inc(taken[name], 1)
                        dve.wait_ge(taken["pr01"], b.at + 1)
                        dve.wait_ge(taken["pr2"], b.at + 1)
                        statistics(h2, stats2, mv2, b, stats2_ready, mv2_ready)
                    elif name == "rt":
                        dve.wait_ge(made[name], b.at + 1)
                        dve.tensor_tensor(logit[:], db[:, 0:EXPERTS], brt[:], ALU.add).then_inc(taken[name], 1)
                        dve.wait_ge(taken[name], b.at + 1)
                        dve.sem_inc(passed["dve"], 1)
                        dve.max(top[:], logit[:]).then_inc(top_ready, 1)
                        dve.wait_ge(top_ready, b.at + 1)
                        dve.sem_inc(passed["dve"], 1)
                        dve.max_index(topi[:], top[:], logit[:]).then_inc(topi_ready, 1)
                        dve.tensor_scalar(shifted[:], logit[:], top[:, 0:1], None, ALU.subtract).then_inc(shifted_ready, 1)
                    elif name == "fu01":
                        dve.wait_ge(made[name], b.at + 1)
                        need(dve, stored, 32 * b.at)
                        dve.scalar_tensor_tensor(ob[:, 0:2, :], db[:].rearrange("p (t n) -> p t n", t=2), gate[:], h2[:, 0:2, :],
                                                 ALU.mult, ALU.add).then_inc(taken[name], 1)
                    elif name == "fu2":
                        dve.wait_ge(made[name], b.at + 1)
                        dve.scalar_tensor_tensor(ob[0:TXT, 2, :], db[0:TXT, 0:D], gate[0:TXT], h2[0:TXT, 2, :],
                                                 ALU.mult, ALU.add).then_inc(taken[name], 1)

                def keys_of_head(b, hd):
                    c, r = hd // 8, hd % 8
                    rows = slice(32 * (r // 2), 32 * (r // 2) + 32)
                    if r == 0:
                        dve.wait_ge(taken[f"k{c}"], b.at + 1)
                    dve.tensor_scalar(km[b.par][rows, hd, :, 0:SEQ], ks[rows, c, :, :], halves[rows, r:r + 1], None,
                                      ALU.mult).then_inc(km_ready, 1)

                def maxima(m, e, j):
                    b, jb = score_job(m, e, j)
                    if not live(b):
                        return
                    c = 2 * (jb % 4)
                    rows = mx[jb // 4]
                    dve.wait_ge(sc_ready, JOBS * b.at + jb + 1)
                    dve.reduce_max(rows[:, 2, c:c + 2], sc[:, 0:2, 0:W0], AX.X).then_inc(mx_ready, 1)
                    dve.reduce_max(rows[0:TXT, 0, c:c + 2], sc[0:TXT, 0:2, W0:W0 + W2], AX.X).then_inc(mx_ready, 1)
                    dve.reduce_max(rows[:, 1, c:c + 2], sc[:, 2, 0:2 * W1].rearrange("p (a c) -> p a c", a=2),
                                   AX.X).then_inc(mx_ready, 1)

                def body(m, e):
                    for j in range(JOBS):
                        slices = [(n, batch(m, e + d)) for n, d in STEPS[j]]
                        for k, (n, b) in enumerate(slices):
                            if k == 2:
                                maxima(m, e, j)
                            if live(b):
                                take(n, b)
                        b = batch(m, e + 1)
                        if live(b) and 2 <= j <= 5:
                            for hd in range(4 * (j - 2), 4 * (j - 2) + 4):
                                keys_of_head(b, hd)
                        if len(slices) < 3:
                            maxima(m, e, j)
                        b = batch(m, e - 2)
                        if j == 1 and live(b):
                            dve.wait_ge(esum_ready, b.at + 1)
                            dve.reciprocal(gate[:], esum[:]).then_inc(gate_ready, 1)
                        if j == 2 and live(b):
                            dve.wait_ge(gate_ready, b.at + 1)
                            dve.sem_inc(passed["dve"], 1)
                        b = batch(m, e + 2)
                        if j == 4 and live(b):
                            first_norm_stats(b)
                        if j == 6 and live(b):
                            normalise(xn, h, mv, rstd1, b, rstd_ready, xn_ready)
                        b = batch(m, e - 1)
                        if j == 6 and live(b):
                            normalise(zn, h2, mv2, rstd2, b, rstd2_ready, zn_ready)
                        if j == 7 and live(b):
                            dve.wait_ge(taken["zt1"], b.at + 1)
                            dve.tensor_tensor(zb[:], zsum[:], bns[:], ALU.mult).then_inc(zb_mul, 1)
                            dve.wait_ge(zb_mul, b.at + 1)
                            dve.tensor_tensor(zb[:], zb[:], bnt[:], ALU.add).then_inc(zb_ready, 1)

                first_norm_stats(batch(0, 0))
                normalise(xn, h, mv, rstd1, batch(0, 0), rstd_ready, xn_ready)
                iterations(dve, body)

            @block.tensor
            def _(pe):
                pe.wait_ge(pool_set, NEED_POOL)
                pe.wait_ge(dve_set, 1)

                def tile(t):
                    return slice(P * t, min(P * t + P, SEQ))

                def make(name, b, before):
                    if before is not None:
                        pe.wait_ge(taken[before[0]], before[1].at + 1)
                    if name in ("xt0", "xt1"):
                        c = int(name[2])
                        pe.wait_ge(xn_ready, 3 * b.at + 3)
                        for t in range(3):
                            ins = pe.transpose(db[:, P * t:P * t + P], xn[:, t, P * c:P * c + P], ident[:])
                    elif name in ("q0", "q1", "k0", "k1"):
                        col = (D if name[0] == "k" else 0) + P * int(name[1])
                        for c in range(CD):
                            ins = pe.matmul(db[:, 0:SEQ], wa[:, c, col:col + P], xnt[:, c, :], start=c == 0, stop=c == CD - 1)
                    elif name in ("v01", "v2"):
                        for n, t in enumerate((0, 1) if name == "v01" else (2,)):
                            k = tile(t)
                            for c in range(CD):
                                ins = pe.matmul(db[0:k.stop - k.start, D * n:D * n + D], xnt[:, c, k], wa[:, c, 2 * D:3 * D],
                                                start=c == 0, stop=c == CD - 1)
                    elif name in ("nm0", "nm1"):
                        u = int(name[2])
                        pe.wait_ge(mx_ready, 3 * (JOBS * b.at + 4 * u + 4))
                        for t, (q0, q1) in enumerate(QT):
                            n = q1 - q0
                            ins = pe.transpose(db[:, q0:q1], mx[u][0:n, t, :], ident[0:n, 0:n])
                    elif name in ("ot0", "ot1", "ot2"):
                        k = tile(int(name[2]))
                        pe.wait_ge(ot_taken, 4 * b.at + 4)
                        for g in range(4):
                            ins = pe.transpose(db[0:k.stop - k.start, P * g:P * g + P], ot[b.par][:, g, k], ident[:])
                    elif name in ("ox0", "ox1"):
                        c = int(name[2])
                        for t in range(3):
                            k = tile(t)
                            n = k.stop - k.start
                            ins = pe.transpose(db[:, k], on[0:n, t, P * c:P * c + P], ident[0:n, 0:n])
                    elif name in ("pr01", "pr2"):
                        for n, t in enumerate((0, 1) if name == "pr01" else (2,)):
                            k = tile(t)
                            for c in range(CD):
                                ins = pe.matmul(db[0:k.stop - k.start, D * n:D * n + D], ont[:, c, k], wp[:, c, :],
                                                start=c == 0, stop=c == CD - 1)
                    elif name in ("zt0", "zt1"):
                        c = int(name[2])
                        pe.wait_ge(zn_ready, 3 * b.at + 3)
                        for t in range(3):
                            k = tile(t)
                            n = k.stop - k.start
                            ins = pe.transpose(db[:, k], zn[0:n, t, P * c:P * c + P], ident[0:n, 0:n])
                    elif name == "rt":
                        pe.wait_ge(zb_ready, b.at + 1)
                        for c in range(CD):
                            ins = pe.matmul(db[:, 0:EXPERTS], zb[:, c:c + 1].broadcast_to([P, P]), wrt[:, c, :],
                                            start=c == 0, stop=c == CD - 1)
                    elif name == "fd":
                        pe.wait_ge(expert_in, 64 * b.at + 64)
                        for c in range(CD):
                            ins = pe.matmul(db[0:HID, 0:SEQ], wd[:, c, :], zt[:, c, :], start=c == 0, stop=c == CD - 1)
                    elif name in ("fu01", "fu2"):
                        for n, t in enumerate((0, 1) if name == "fu01" else (2,)):
                            k = tile(t)
                            ins = pe.matmul(db[0:k.stop - k.start, D * n:D * n + D], hid[:, k], wu[:], start=True, stop=True)
                    ins.then_inc(made[name], 1)

                def scores_t(b, j, a):
                    hd = 2 * j + a
                    c = hd // 8
                    if a == 0:
                        if j % 4 == 0:
                            pe.wait_ge(taken[f"nm{j // 4}"], b.at + 1)
                        need(pe, exp_done, 2 * (JOBS * b.at + j))
                    for (k0, q0), o in zip(KT, (st[:, a, 0:W0], st[:, 2, W1 * a:W1 * a + W1], st[:, a, W0:W0 + W2])):
                        pe.matmul(o, pick[:, hd % 8, :], nmt[c][:, q0:SEQ], start=True, stop=False)
                        for kp, qp in ((0, 0), (0, 1), (1, 0)):
                            ins = pe.matmul(o, km[b.par][:, hd, kp, k0:k0 + P], qs[b.par][:, c, qp, q0:SEQ],
                                            start=False, stop=kp == 1)
                    if a == 1:
                        ins.then_inc(st_ready, 1)

                def scores(b, j):
                    pe.wait_ge(km_ready, HEADS * b.at + 2 * j + 2)
                    need(pe, mx_ready, 3 * (JOBS * b.at + j))
                    for a in range(2):
                        hd = 2 * j + a
                        for (q0, q1), o in zip(QT, (sc[0:TXT, a, W0:W0 + W2], sc[:, 2, W1 * a:W1 * a + W1], sc[:, a, 0:W0])):
                            n = q1 - q0
                            pe.matmul(o[:, q0:q1], ident16[:, 0:n], later[:, 0:n], start=True, stop=False, skip_group_check=True)
                            ins = pe.matmul(o, qs[b.par][:, hd // 8, 0, q0:q1], km[b.par][:, hd, 0, 0:q1],
                                            start=False, stop=True, skip_group_check=True)
                    ins.then_inc(sc_ready, 1)

                def values(b, g):
                    pe.wait_ge(causal, 3 * (JOBS * b.at + 2 * g + 2))
                    need(pe, ot_taken, 4 * b.at + g)
                    pe.sem_inc(passed["pe"], 1)
                    for n, (_, q0) in enumerate(KT):
                        for a in range(4):
                            p = pr[(2 * g + a // 2) % PSLOTS]
                            aa = a % 2
                            src = (p[:, aa, 0:W0], p[:, 2, W1 * aa:W1 * aa + W1], p[:, aa, W0:W0 + W2])[n]
                            ins = pe.matmul(otp[32 * a:32 * a + 32, q0:SEQ], v[b.par][:, n, 4 * g + a, :], src,
                                            start=n == 0, stop=n == 2)
                    ins.then_inc(pv_done, 1)

                def body(m, e):
                    now = batch(m, e)
                    for j in range(JOBS):
                        at = sum(len(s) for s in STEPS[:j])
                        for k in range(3):
                            if k < 2 and live(now):
                                scores_t(now, j, k)
                            if k == 2:
                                b, jb = score_job(m, e, j)
                                if live(b):
                                    scores(b, jb)
                            if k < len(STEPS[j]):
                                name, d = STEPS[j][k]
                                b = batch(m, e + d)
                                if live(b):
                                    make(name, b, slice_before(m, e, at + k))
                        g = pv_group(m, e, j)
                        if g is not None:
                            values(*g)

                iterations(pe, body)


_INS = ['x', 'txt', 'L0_tok_log_dt', 'L0_tok_inv_A_real', 'L0_tok_A_imag', 'L0_tok_B_ri', 'L0_attn_w_attn',
        'L0_attn_b_attn', 'L0_attn_w_proj', 'L0_attn_b_proj', 'L0_ffn_ln_g', 'L0_ffn_ln_b', 'L0_ffn_bn_g',
        'L0_ffn_bn_b', 'L0_ffn_bn_mean', 'L0_ffn_bn_var', 'L0_ffn_Wr', 'L0_ffn_br', 'L0_ffn_W_down',
        'L0_ffn_b_down', 'L0_ffn_W_up', 'L0_ffn_b_up']


def kernel(**inputs):
    import numpy as _np
    import concourse.bacc as _bacc
    from concourse import mybir as _mybir
    from concourse.bass_utils import run_bass_kernel_spmd as _run

    nc = _bacc.Bacc("TRN2", target_bir_lowering=False, num_devices=1)
    arrays, args = {}, []
    for name in _INS:
        a = _np.ascontiguousarray(inputs[name])
        arrays[f"in_{name}_dram"] = a
        args.append(nc.dram_tensor(f"in_{name}_dram", a.shape, _mybir.dt.from_np(a.dtype), kind="ExternalInput").ap())
    out = nc.dram_tensor("out_0_dram", (32, 333, 256), _mybir.dt.float32, kind="ExternalOutput").ap()
    scratch = nc.dram_tensor("token_scratch", (32, 256, 256), _mybir.dt.float32, kind="Internal").ap()
    x, txt, log_dt, inv_a, a_imag, b_ri = args[:6]
    build_tokens(nc, x, log_dt, inv_a, a_imag, b_ri, scratch)
    build_layer(nc, scratch, txt, *args[6:], out)
    r = _run(nc, [arrays], core_ids=[0])
    return r.results[0]["out_0_dram"]
```

```python
import concourse.bass as bass
from concourse import mybir
from collections import namedtuple
from contextlib import ExitStack

F32 = mybir.dt.float32
F16 = mybir.dt.float16
BF16 = mybir.dt.bfloat16
U32 = mybir.dt.uint32
ALU = mybir.AluOpType
ACT = mybir.ActivationFunctionType
AX = mybir.AxisListType

P = 128
BATCH, HK, NS, D = 32, 256, 64, 256
TXT = 77
SEQ = HK + TXT
SEQP = 3 * P
HEADS, DH = 16, 16
EXPERTS, HID = 8, 64
EPS = 1e-5
CD = D // P
HR = 4 * DH
MASKED = -30000.0
EULER = 2.718281828459045

HP = HK // 2
HPC = 16
CHUNKS = HP // HPC
LV = 128
SQUARINGS = 7

QT = [(0, TXT), (TXT, TXT + P), (TXT + P, SEQ)]
KT = [(0, 0), (P, P), (2 * P, 2 * P)]
W0, W1, W2 = SEQ, SEQ - P, SEQ - 2 * P


def build_tokens(nc, x, log_dt, inv_a, a_imag, b_ri, scratch):
    x_v = x.rearrange("c (h q) n r -> c h (q n r)", q=2)
    scr_v = scratch.rearrange("c (h q) l -> q c h l", q=2)
    ctx = ExitStack()
    with ctx:
        def sb(name, shape, dt=F32):
            return ctx.enter_context(nc.sbuf_tensor(name, shape, dt))

        def sem(name):
            return ctx.enter_context(nc.semaphore(name))

        ident = sb("ident1", [P, P])
        ld = sb("ld", [P, 2])
        ia = sb("ia", [P, 2, NS])
        ai = sb("ai", [P, 2, NS])
        braw = sb("braw", [P, 2, NS, 2])
        euler = sb("euler", [P, 2 * NS])
        dt = sb("dt", [P, 2])
        decay = sb("decay", [P, 2, NS])
        wr = sb("wr", [P, 2, NS])
        wi = sb("wi", [P, 2, NS])
        sq = sb("sq", [P, 2, NS])
        den = sb("den", [P, 2, NS])
        pre = sb("pre", [P, 4, 2, NS])
        bt = sb("bt", [P, 2, HP])
        zr = sb("zr", [P, SQUARINGS + 1, HP])
        zi = sb("zi", [P, SQUARINGS + 1, HP])
        nzi = sb("nzi", [P, SQUARINGS + 1, HP])
        dif = sb("dif", [P, HP])
        tot = sb("tot", [P, HP])
        xin = [sb(f"xin{q}", [P, 4, 4 * NS]) for q in range(2)]
        a = [sb(f"c{q}", [P, 2, HPC, 2, BATCH]) for q in range(2)]
        v = [sb(f"powers{q}", [P, 2, HPC, LV]) for q in range(2)]
        vtmp = sb("vtmp", [P, 2, HPC, LV // 2])
        atmp = sb("atmp", [P, 2, HPC, BATCH])
        hst = [sb(f"hst{q}", [P, HPC, LV]) for q in range(2)]
        tp = ctx.enter_context(nc.psum_tensor("tp", [P, 2, 512], F32))
        kp = [[ctx.enter_context(nc.psum_tensor(f"kp{q}{s}", [P, 4, LV], F32)) for s in range(2)] for q in range(2)]

        par_in = sem("par_in")
        ident_set = sem("ident_set")
        euler_set = sem("euler_set")
        pow_done = sem("pow_done")
        link = sem("param_link")
        pre_ready = sem("pre_ready")
        pre_t = sem("pre_transposed")
        bt_ready = sem("bt_ready")
        z_link = sem("z_link")
        z_ready = sem("z_ready")
        xin_in = [sem(f"xin_in{q}") for q in range(2)]
        ct_ready = sem("ct_ready")
        a0_ready = sem("a0_ready")
        a1_mul = sem("a1_mul")
        a1_ready = sem("a1_ready")
        v_link = sem("v_link")
        v_ready = sem("v_ready")
        k_ready = sem("k_ready")
        k_taken = sem("k_taken")
        hst_out = [sem(f"hst_out{q}") for q in range(2)]
        pool_passed = sem("pool_passed1")
        sp_passed = sem("sp_passed1")
        pe_passed = sem("pe_passed1")

        LINKS = 1 + 4 * SQUARINGS

        def chunks(eng, body):
            body(0, 0, 0)
            body(1, 0, 1)
            with eng.Fori(1, CHUNKS // 2 - 1) as m:
                body(2 * m, m, 0)
                body(2 * m + 1, m, 1)
            body(CHUNKS - 2, CHUNKS // 2 - 1, 0)
            body(CHUNKS - 1, CHUNKS // 2 - 1, 1)

        def first(k):
            return isinstance(k, int) and k < 2

        def last(k):
            return isinstance(k, int) and k == CHUNKS - 1

        with nc.Block() as block:

            @block.sync
            def _(sp):
                sp.dma_start(ld[:], log_dt.rearrange("(h q) -> h q", q=2)).then_inc(par_in, 16)
                sp.dma_start(ia[:], inv_a.rearrange("(h q) n -> h q n", q=2)).then_inc(par_in, 16)
                sp.dma_start(ai[:], a_imag.rearrange("(h q) n -> h q n", q=2)).then_inc(par_in, 16)
                sp.dma_start(braw[:], b_ri.rearrange("(h q) n r -> h q n r", q=2)).then_inc(par_in, 16)

                def body(k, m, q):
                    if not first(k):
                        sp.wait_ge(ct_ready, k - 1)
                        sp.sem_inc(sp_passed, 1)
                    for t in range(4):
                        sp.dma_start(xin[q][:, t, :], x_v[8 * t:8 * t + 8, bass.ds(HPC * k, HPC), :]).then_inc(xin_in[q], 16)
                    if not (isinstance(k, int) and k == 0):
                        store(k - 1, 1 - q)

                def store(k, q):
                    sp.wait_ge(k_taken, 8 * k + 8)
                    sp.sem_inc(sp_passed, 1)
                    for par in range(2):
                        for i in range(2):
                            p0 = 64 * par + 32 * i
                            sp.dma_start(scr_v[par, :, bass.ds(HPC * k, HPC), i * LV:(i + 1) * LV],
                                         hst[q][p0:p0 + 32, :, :]).then_inc(hst_out[q], 16)

                chunks(sp, body)
                store(CHUNKS - 1, 1)
                for q in range(2):
                    sp.wait_ge(hst_out[q], 64 * (CHUNKS // 2))

            @block.gpsimd
            def _(pool):
                pool.memset(ident[:], 0.0).then_inc(ident_set, 1)
                pool.memset(euler[:], EULER).then_inc(euler_set, 1)
                pool.wait_ge(ident_set, 1)
                pool.affine_select(out=ident[:], in_=ident[:], compare_op=ALU.not_equal, fill=1.0, base=0,
                                   pattern=[[-1, P]], channel_multiplier=1).then_inc(ident_set, 1)
                pool.wait_ge(euler_set, 1)
                pool.wait_ge(par_in, 64)
                pool.tensor_tensor(dt[:], euler[:, 0:2], ld[:], ALU.pow).then_inc(pow_done, 1)
                pool.tensor_tensor(decay[:].rearrange("p q n -> p (q n)"), euler[:],
                                   ia[:].rearrange("p q n -> p (q n)"), ALU.pow).then_inc(pow_done, 1)

                def body(k, m, q):
                    if isinstance(k, int) and k == 0:
                        pool.wait_ge(z_ready, 1)
                    pool.wait_ge(a0_ready, 2 * k + 2)
                    hs = bass.ds(HPC * k, HPC)

                    def zb(z):
                        return z[:, SQUARINGS, hs].unsqueeze(2).broadcast_to([P, HPC, BATCH])

                    src = a[q][:, :, :, 0, :]
                    dst = a[q][:, :, :, 1, :]
                    pool.tensor_tensor(dst[:, 0], src[:, 0], zb(zr), ALU.mult).then_inc(a1_mul, 1)
                    pool.tensor_tensor(dst[:, 1], src[:, 1], zb(zr), ALU.mult).then_inc(a1_mul, 1)
                    if not (isinstance(k, int) and k == 0):
                        pool.wait_ge(a1_ready, k)
                    pool.tensor_tensor(atmp[:, 0], src[:, 1], zb(zi), ALU.mult).then_inc(a1_mul, 1)
                    pool.tensor_tensor(atmp[:, 1], src[:, 0], zb(nzi), ALU.mult).then_inc(a1_mul, 1)
                    pool.wait_ge(a1_mul, 4 * k + 4)
                    pool.tensor_tensor(dst, dst, atmp[:], ALU.add).then_inc(a1_ready, 1)

                chunks(pool, body)

            @block.scalar
            def _(act):
                act.wait_ge(z_link, 2)
                act.copy(bt[:, :, :], tp[:, 0, 256:512].rearrange("p (r h) -> p r h", r=2)).then_inc(bt_ready, 1)

                def take_c(k, q):
                    act.wait_ge(ct_ready, k + 1)
                    if not first(k):
                        act.wait_ge(k_ready, 4 * k - 4)
                    for ri in range(2):
                        act.mul(a[q][:, ri, :, 0, :].rearrange("p h c -> p c h"),
                                tp[:, ri, :].rearrange("p (c h) -> p c h", h=HPC),
                                1.0 - 2.0 * ri).then_inc(a0_ready, 1)

                take_c(0, 0)

                def body(k, m, q):
                    if not last(k):
                        take_c(k + 1, 1 - q)
                    if not first(k):
                        act.wait_ge(hst_out[q], 64 * m)
                    for g in range(4):
                        act.wait_ge(k_ready, 4 * k + g + 1)
                        for par in range(2):
                            rows = slice(64 * par, 64 * par + 64)
                            act.copy(hst[q][rows, 4 * g:4 * g + 4, :], kp[par][g % 2][rows, :, :]).then_inc(k_taken, 1)

                chunks(act, body)

            @block.vector
            def _(dve):
                n = [0]

                def step(ins):
                    n[0] += 1
                    ins.then_inc(link, 1)

                def done():
                    dve.wait_ge(link, n[0])

                dve.wait_ge(pow_done, 2)
                dve.wait_ge(par_in, 64)
                dtb = dt[:].unsqueeze(2).broadcast_to([P, 2, NS])
                step(dve.scalar_tensor_tensor(wr[:], decay[:], -0.5, dtb, ALU.mult, ALU.mult))
                step(dve.scalar_tensor_tensor(wi[:], ai[:], 0.5, dtb, ALU.mult, ALU.mult))
                done()
                step(dve.tensor_scalar(sq[:], wr[:], -1.0, 1.0, ALU.mult, ALU.add))
                step(dve.tensor_tensor(tot[:].rearrange("p (q n) -> p q n", q=2), wi[:], wi[:], ALU.mult))
                done()
                wi2 = tot[:].rearrange("p (q n) -> p q n", q=2)
                step(dve.tensor_tensor(den[:], sq[:], sq[:], ALU.mult))
                step(dve.scalar_tensor_tensor(pre[:, 0], wr[:], 1.0, sq[:], ALU.add, ALU.mult))
                done()
                step(dve.tensor_tensor(den[:], den[:], wi2, ALU.add))
                step(dve.tensor_tensor(pre[:, 0], pre[:, 0], wi2, ALU.subtract))
                done()
                step(dve.reciprocal(den[:], den[:]))
                done()
                dve.tensor_tensor(pre[:, 0], pre[:, 0], den[:], ALU.mult).then_inc(pre_ready, 1)
                dve.scalar_tensor_tensor(pre[:, 1], wi[:], 2.0, den[:], ALU.mult, ALU.mult).then_inc(pre_ready, 1)
                dve.tensor_scalar(pre[:, 2], braw[:, :, :, 0], 2.0, None, ALU.mult).then_inc(pre_ready, 1)
                dve.tensor_scalar(pre[:, 3], braw[:, :, :, 1], 2.0, None, ALU.mult).then_inc(pre_ready, 1)
                dve.wait_ge(pre_t, 1)
                c = 0

                def zstep(ins):
                    ins.then_inc(z_link, 1)

                zstep(dve.tensor_copy(zr[:, 0, :], tp[:, 0, 0:P]))
                zstep(dve.tensor_copy(zi[:, 0, :], tp[:, 0, P:2 * P]))
                c += 2
                for k in range(SQUARINGS):
                    dve.wait_ge(z_link, c)
                    zstep(dve.tensor_tensor(dif[:], zr[:, k], zi[:, k], ALU.subtract))
                    zstep(dve.tensor_tensor(tot[:], zr[:, k], zi[:, k], ALU.add))
                    zstep(dve.scalar_tensor_tensor(zi[:, k + 1], zr[:, k], 2.0, zi[:, k], ALU.mult, ALU.mult))
                    c += 3
                    dve.wait_ge(z_link, c)
                    zstep(dve.tensor_tensor(zr[:, k + 1], dif[:], tot[:], ALU.mult))
                    c += 1
                dve.wait_ge(z_link, c)
                zstep(dve.tensor_scalar(nzi[:], zi[:], -1.0, None, ALU.mult))
                c += 1
                dve.wait_ge(z_link, c)
                dve.tensor_copy(dif[:, 0:1], dt[:, 0:1]).then_inc(z_ready, 1)

                def body(k, m, q):
                    hs = bass.ds(HPC * k, HPC)
                    base = LINKS * k
                    if isinstance(k, int) and k == 0:
                        dve.wait_ge(bt_ready, 1)
                    if not first(k):
                        dve.wait_ge(k_ready, 4 * k - 4)
                    dve.tensor_copy(v[q][:, :, :, 0:1], bt[:, :, hs].unsqueeze(3)).then_inc(v_link, 1)
                    c = 1
                    for s in range(SQUARINGS):
                        w = 1 << s

                        def zb(z):
                            return z[:, s, hs].unsqueeze(2).broadcast_to([P, HPC, w])

                        lo = v[q][:, :, :, 0:w]
                        hi = v[q][:, :, :, w:2 * w]
                        tmp = vtmp[:, :, :, 0:w]
                        dve.wait_ge(v_link, base + c)
                        dve.tensor_tensor(tmp[:, 0], lo[:, 1], zb(nzi), ALU.mult).then_inc(v_link, 1)
                        dve.tensor_tensor(tmp[:, 1], lo[:, 0], zb(zi), ALU.mult).then_inc(v_link, 1)
                        dve.tensor_tensor(hi, lo, z_both(s, hs, w), ALU.mult).then_inc(v_link, 1)
                        c += 3
                        dve.wait_ge(v_link, base + c)
                        ins = dve.tensor_tensor(hi, hi, tmp, ALU.add)
                        c += 1
                        if s == SQUARINGS - 1:
                            ins.then_inc(v_ready, 1)
                            dve.sem_inc(v_link, 1)
                        else:
                            ins.then_inc(v_link, 1)

                def z_both(s, hs, w):
                    return zr[:, s, hs].unsqueeze(1).unsqueeze(3).broadcast_to([P, 2, HPC, w])

                chunks(dve, body)

            @block.tensor
            def _(pe):
                pe.wait_ge(ident_set, 2)
                pe.wait_ge(pre_ready, 4)
                for j in range(4):
                    ins = pe.transpose(tp[:, 0, P * j:P * j + P], pre[:, j].rearrange("p q n -> p (q n)"), ident[:])
                ins.then_inc(pre_t, 1)
                pe.wait_ge(bt_ready, 1)
                pe.wait_ge(z_link, 2)

                def turn_c(k, m, q):
                    pe.wait_ge(xin_in[q], 64 * m + 64)
                    if not (isinstance(k, int) and k == 0):
                        pe.wait_ge(a0_ready, 2 * k)
                    for ri in range(2):
                        for t in range(4):
                            src = xin[q][:, t, :].rearrange("p (f r) -> p r f", r=2)[:, ri, :]
                            ins = pe.transpose(tp[:, ri, P * t:P * t + P], src, ident[:])
                    ins.then_inc(ct_ready, 1)

                turn_c(0, 0, 0)

                def body(k, m, q):
                    if not last(k):
                        turn_c(k + 1, m if q == 0 else m + 1, 1 - q)
                    pe.wait_ge(v_ready, k + 1)
                    pe.wait_ge(a1_ready, k + 1)
                    for g in range(4):
                        if not (isinstance(k, int) and k == 0 and g < 2):
                            pe.wait_ge(k_taken, 8 * k + 2 * g - 2)
                        pe.sem_inc(pe_passed, 1)
                        for h in range(4 * g, 4 * g + 4):
                            for par in range(2):
                                rows = slice(64 * par, 64 * par + 64)
                                for ri in range(2):
                                    ins = pe.matmul(kp[par][g % 2][rows, h % 4, :],
                                                    a[q][rows, ri, h, :, :].rearrange("p i c -> p (i c)"),
                                                    v[q][rows, ri, h, :], start=ri == 0, stop=ri == 1)
                        ins.then_inc(k_ready, 1)

                chunks(pe, body)


STEPS = [
    ["st0", ("xt0", 1, 0), "st1", ("xt1", 1, 1), "sc", ("rt", -2, 0), ("pv3", -1, 1)],
    ["st0", ("q0", 1, 0), "st1", ("k0", 1, 1), "sc", ("q1", 1, 0)],
    ["st0", ("k1", 1, 1), "st1", ("fd", -2, 0), "sc", ("pv0", 0, 1)],
    ["st0", ("nm1", 0, 1), "st1", ("fu01", -2, 0), "sc", ("fu2", -2, 1)],
    ["st0", ("ot0", -1, 0), "st1", ("ot1", -1, 1), "sc", ("ot2", -1, 0), ("pv1", 0, 1)],
    ["st0", ("ox0", -1, 0), "st1", ("ox1", -1, 1), "sc", ("pr01", -1, 0), ("pr2", -1, 1)],
    ["st0", "st1", ("v01", 1, 0), "sc", ("pv2", 0, 1)],
    ["st0", ("nm0", 1, 0), "st1", ("v2", 1, 1), "sc", ("zt0", -1, 0), ("zt1", -1, 1)],
]
SLICES = [x for step in STEPS for x in step if not isinstance(x, str)]
ACT_TAKES = ("xt0", "xt1", "q0", "q1", "k0", "k1", "nm0", "nm1", "ox0", "ox1", "zt0", "zt1", "rt", "fd",
             "pv0", "pv1", "pv2", "pv3")
JOBS = 8
PSLOTS = 4
Batch = namedtuple("Batch", "at half par")


def batch(m, e):
    return Batch(2 * m + e, m + e // 2, e % 2)


def live(b):
    return not isinstance(b.at, int) or 0 <= b.at < BATCH


def iterations(eng, body):
    for i in range(-1, 3):
        body(0, i)
    with eng.Fori(1, BATCH // 2 - 2) as m:
        body(m, 1)
        body(m, 2)
    for i in range(BATCH - 3, BATCH + 2):
        body(0, i)


def need(eng, sem, count):
    if not isinstance(count, int) or count > 0:
        eng.wait_ge(sem, count)


def score_job(m, e, j):
    return (batch(m, e + 1), j - 3) if j >= 3 else (batch(m, e), j + 5)


def slice_before(m, e, name):
    k = [x[0] for x in SLICES].index(name)
    bank = SLICES[k][2]
    while True:
        k -= 1
        if k < 0:
            k += len(SLICES)
            e -= 1
        if e < -1 and isinstance(m, int):
            return None
        other, d, its = SLICES[k]
        if its == bank and live(batch(m, e + d)):
            return other, batch(m, e + d)


def build_layer(nc, scratch, txt, w_attn, b_attn, w_proj, b_proj, ln_g, ln_b, bn_g, bn_b, bn_mean, bn_var,
                w_r, b_r, w_down, b_down, w_up, b_up, out):
    ctx = ExitStack()
    with ctx:
        def sb(name, shape, dt=F32):
            return ctx.enter_context(nc.sbuf_tensor(name, shape, dt))

        def sem(name):
            return ctx.enter_context(nc.semaphore(name))

        ident = sb("ident", [P, P])
        ident16 = sb("ident16", [P, P], BF16)
        later = sb("later", [P, P], BF16)
        minus_half = sb("minus_half", [P, 4])
        band = sb("band", [P, 8])
        band2 = sb("band2", [P, 4])
        wa = sb("wa", [P, CD, 3 * D])
        wp = sb("wp", [P, CD, D])
        wrt = sb("wrt", [P, CD, EXPERTS])
        bqk = sb("bqk", [HR, 8])
        wah = sb("wah", [P, CD, 3 * D], F16)
        wal = sb("wal", [P, CD, 3 * D], F16)
        bv = sb("bv", [P, HEADS, DH])
        bp = sb("bp", [P, D])
        brt = sb("brt", [P, EXPERTS])
        lng = sb("lng", [P, CD])
        lnb = sb("lnb", [P, CD])
        bng = sb("bng", [P, CD])
        bnb = sb("bnb", [P, CD])
        bnm = sb("bnm", [P, CD])
        bnv = sb("bnv", [P, CD])
        bns = sb("bns", [P, CD])
        bnt = sb("bnt", [P, CD])
        h = sb("h", [P, 3, D])
        stats = sb("stats", [P, 3, 6])
        mv = sb("mv", [P, 3, 2])
        var1 = sb("var1", [P, 3])
        rstd1 = sb("rstd1", [P, 3])
        xn = sb("xn", [P, 3, D])
        xh = sb("xh", [P, CD, SEQ], F16)
        xl = sb("xl", [P, CD, SEQ], F16)
        qa = [sb(f"qa{q}", [P, 4, SEQ], F16) for q in range(2)]
        qb = [sb(f"qb{q}", [P, 4, SEQ], F16) for q in range(2)]
        kh = sb("kh", [P, 4, SEQ], F16)
        kl = sb("kl", [HR, 4, SEQ], F16)
        ka = [sb(f"ka{q}", [P, HEADS, SEQP], F16) for q in range(2)]
        kb = [sb(f"kb{q}", [P, HEADS, SEQP], F16) for q in range(2)]
        v = [sb(f"v{q}", [P, 3, HEADS, 2 * DH]) for q in range(2)]
        mx = [sb(f"mx{u}", [P, 3, P]) for u in range(2)]
        pr = [sb(f"pr{s}", [P, 3, W0 + W2]) for s in range(PSLOTS)]
        ot = [sb(f"ot{q}", [P, 4, SEQ]) for q in range(2)]
        rden = sb("rden", [P, 3, HEADS])
        on = sb("on", [P, 3, D])
        ont = sb("ont", [P, CD, SEQ])
        res = sb("res", [P, 3, D])
        h2 = sb("h2", [P, 3, D])
        stats2 = sb("stats2", [P, 3, 6])
        mv2 = sb("mv2", [P, 3, 2])
        var2 = sb("var2", [P, 3])
        rstd2 = sb("rstd2", [P, 3])
        zn = sb("zn", [P, 3, D])
        zt = sb("zt", [P, CD, SEQ])
        zsum = sb("zsum", [P, CD])
        zb = sb("zb", [P, CD])
        logit = sb("logit", [P, EXPERTS])
        top = sb("top", [P, 8])
        topi = sb("topi", [P, 8], U32)
        shifted = sb("shifted", [P, EXPERTS])
        expd = sb("expd", [P, EXPERTS])
        esum = sb("esum", [P, 1])
        gate = sb("gate", [P, 1])
        wd = sb("wd", [P, CD, HID])
        wu = sb("wu", [HID + 1, D])
        bd = sb("bd", [HID, 1])
        hid = sb("hid", [HID + 1, SEQ])
        ob = sb("ob", [P, 3, D])

        st = ctx.enter_context(nc.psum_tensor("st", [P, 3, 512], F32))
        sc = ctx.enter_context(nc.psum_tensor("sc", [P, 3, 512], F32))
        banks = [ctx.enter_context(nc.psum_tensor(f"shared{q}", [P, 512], F32)) for q in range(2)]
        bank_of = {n: banks[q] for n, _, q in SLICES}

        weights_in = sem("weights_in")
        pool_set = sem("pool_set")
        dve_set = sem("dve_set")
        setup_done = sem("setup_done")
        made = {n: sem(f"made_{n}") for n, _, _ in SLICES}
        taken = {n: sem(f"taken_{n}") for n, _, _ in SLICES}
        h_in = sem("h_in")
        stats_ready = sem("stats_ready")
        mv_ready = sem("mv_ready")
        var_ready = sem("var_ready")
        rstd_ready = sem("rstd_ready")
        xn_ready = sem("xn_ready")
        qh_ready = sem("qh_ready")
        kh_ready = sem("kh_ready")
        xh_ready = sem("xh_ready")
        nm_half = sem("nm_half")
        kh_twice = [sem(f"kh_twice{c}") for c in range(2)]
        qh_twice = sem("qh_twice")
        km_ready = sem("km_ready")
        sc_ready = sem("sc_ready")
        mx_ready = sem("mx_ready")
        st_ready = sem("st_ready")
        exp_done = sem("exp_done")
        causal = sem("causal")
        rden_ready = sem("rden_ready")
        res_in = sem("res_in")
        res_ready = sem("res_ready")
        stats2_ready = sem("stats2_ready")
        mv2_ready = sem("mv2_ready")
        var2_ready = sem("var2_ready")
        rstd2_ready = sem("rstd2_ready")
        zn_ready = sem("zn_ready")
        zb_mul = sem("zb_mul")
        zb_ready = sem("zb_ready")
        top_ready = sem("top_ready")
        topi_ready = sem("topi_ready")
        shifted_ready = sem("shifted_ready")
        esum_ready = sem("esum_ready")
        gate_ready = sem("gate_ready")
        expert_in = sem("expert_in")
        stored = sem("stored")
        passed = {n: sem(f"passed_{n}") for n in ("sp", "pool", "dve", "pe")}

        NEED_POOL = 15

        with nc.Block() as block:

            @block.sync
            def _(sp):
                col = "(c p) -> p c"
                sp.dma_start(wa[:], w_attn.rearrange("(c p) n -> p c n", p=P)).then_inc(weights_in, 16)
                sp.dma_start(wp[:], w_proj.rearrange("(c p) n -> p c n", p=P)).then_inc(weights_in, 16)
                sp.dma_start(wrt[:], w_r.rearrange("(c p) n -> p c n", p=P)).then_inc(weights_in, 16)
                sp.dma_start(bqk[:], b_attn[0:2 * D].rearrange("(c r) -> r c", r=HR), allow_slow_non_contiguous=True).then_inc(weights_in, 16)
                sp.dma_start(bv[:].rearrange("p h d -> p (h d)"),
                             b_attn[2 * D:3 * D].unsqueeze(0).broadcast_to([P, D])).then_inc(weights_in, 16)
                sp.dma_start(bp[:], b_proj.unsqueeze(0).broadcast_to([P, D])).then_inc(weights_in, 16)
                sp.dma_start(brt[:], b_r.unsqueeze(0).broadcast_to([P, EXPERTS])).then_inc(weights_in, 16)
                for dst, src in ((lng, ln_g), (lnb, ln_b), (bng, bn_g), (bnb, bn_b), (bnm, bn_mean), (bnv, bn_var)):
                    sp.dma_start(dst[:], src.rearrange(col, p=P), allow_slow_non_contiguous=True).then_inc(weights_in, 16)
                sp.wait_ge(pool_set, NEED_POOL)
                sp.wait_ge(dve_set, 1)

                def load(dst, b, sm):
                    sp.dma_start(dst[:, 0:2, :], scratch[bass.ds(b.at, 1), :, :].rearrange("b (t p) l -> p (b t) l", p=P)).then_inc(sm, 16)
                    sp.dma_start(dst[0:TXT, 2:3, :], txt[bass.ds(b.at, 1), :, :].rearrange("b p l -> p b l")).then_inc(sm, 16)

                def body(m, e):
                    if e == -1:
                        load(h, batch(m, 0), h_in)
                    b = batch(m, e + 2)
                    if live(b):
                        need(sp, xn_ready, 3 * b.at)
                        sp.sem_inc(passed["sp"], 1)
                        load(h, b, h_in)
                    b = batch(m, e - 1)
                    if live(b):
                        need(sp, taken["pr2"], b.at)
                        sp.sem_inc(passed["sp"], 1)
                        load(res, b, res_in)
                    b = batch(m, e - 2)
                    if live(b):
                        sp.wait_ge(topi_ready, b.at + 1)
                        sp.sem_inc(passed["sp"], 1)
                        x = sp.value_load(topi[0:1, 0:1], min_val=0, max_val=EXPERTS - 1)
                        one = bass.ds(x, 1)
                        sp.dma_start(wd[:], w_down[one, :, :].rearrange("e (c p) f -> p (e c) f", p=P)).then_inc(expert_in, 16)
                        sp.dma_start(bd[:], b_down[one, :].rearrange("e f -> f e"), allow_slow_non_contiguous=True).then_inc(expert_in, 16)
                        sp.dma_start(wu[0:HID, :], w_up[one, :, :].rearrange("e f d -> (e f) d")).then_inc(expert_in, 16)
                        sp.dma_start(wu[HID:HID + 1, :], b_up[one, :]).then_inc(expert_in, 16)
                    nxt = batch(m, e + 1)
                    if live(nxt):
                        for c in range(2):
                            sp.wait_ge(kh_ready, 4 * nxt.at + 2 * c + 2)
                            sp.sem_inc(passed["sp"], 1)
                            sp.dma_start(kh[HR:P, 2 * c:2 * c + 2, :], kh[0:HR, 2 * c:2 * c + 2, :]).then_inc(kh_twice[c], 16)
                            if c == 0:
                                sp.wait_ge(qh_ready, 4 * nxt.at + 4)
                                sp.sem_inc(passed["sp"], 1)
                                sp.dma_start(qb[nxt.par][0:HR], qa[nxt.par][0:HR]).then_inc(qh_twice, 16)
                    if live(b):
                        sp.wait_ge(taken["fu2"], b.at + 1)
                        sp.sem_inc(passed["sp"], 1)
                        o = out[bass.ds(b.at, 1), :, :]
                        sp.dma_start(o[:, 0:HK, :].rearrange("b (t p) l -> p (b t) l", p=P), ob[:, 0:2, :]).then_inc(stored, 16)
                        sp.dma_start(o[:, HK:SEQ, :].rearrange("b p l -> p b l"), ob[0:TXT, 2:3, :]).then_inc(stored, 16)

                iterations(sp, body)
                sp.wait_ge(stored, 32 * BATCH)

            @block.gpsimd
            def _(pool):
                pool.memset(ident[:], 0.0).then_inc(pool_set, 1)
                pool.memset(ident16[:], 0.0).then_inc(pool_set, 1)
                pool.memset(later[:], 0.0).then_inc(pool_set, 1)
                pool.memset(minus_half[:], -0.5).then_inc(pool_set, 1)
                pool.memset(band[:], 1.0).then_inc(pool_set, 1)
                pool.wait_ge(pool_set, 5)
                pool.memset(kb[0][HR:P], 1.0).then_inc(pool_set, 1)
                pool.wait_ge(pool_set, 6)
                for t in (ident, ident16):
                    pool.affine_select(out=t[:], in_=t[:], compare_op=ALU.not_equal, fill=1.0, base=0,
                                       pattern=[[-1, P]], channel_multiplier=1).then_inc(pool_set, 1)
                pool.affine_select(out=later[:], in_=later[:], compare_op=ALU.is_ge, fill=MASKED, base=0,
                                   pattern=[[-1, P]], channel_multiplier=1).then_inc(pool_set, 1)
                for q in range(2):
                    pool.wait_ge(pool_set, 9 + q)
                    rows = kb[1 - q][HR:P].rearrange("p (c r) k -> p c r k", r=4)
                    src = kb[0][HR:P].rearrange("p (c r) k -> p c r k", r=4)
                    pool.affine_select(out=rows, in_=src, compare_op=ALU.is_equal, fill=0.0, base=0,
                                       pattern=[[0, 4], [-1, 4], [0, SEQP]], channel_multiplier=1).then_inc(pool_set, 1)
                pool.wait_ge(pool_set, 11)
                pool.affine_select(out=band[:], in_=band[:], compare_op=ALU.is_ge, fill=0.0, base=0,
                                   pattern=[[-DH, 8]], channel_multiplier=1).then_inc(pool_set, 1)
                pool.wait_ge(pool_set, 12)
                pool.affine_select(out=band[:], in_=band[:], compare_op=ALU.is_ge, fill=0.0, base=DH - 1,
                                   pattern=[[DH, 8]], channel_multiplier=-1).then_inc(pool_set, 1)
                pool.wait_ge(dve_set, 1)
                pool.wait_ge(weights_in, 13 * 16)
                pool.tensor_scalar(bns[:], bnv[:], 1.0, EPS, ALU.mult, ALU.add).then_inc(pool_set, 1)
                pool.wait_ge(pool_set, 14)
                pool.tensor_tensor(bns[:], bns[:], minus_half[:, 0:CD], ALU.pow).then_inc(pool_set, 1)

                def power(src, scale, eps, var, rstd, b, got, mid, ready):
                    pool.wait_ge(got, 3 * b.at + 3)
                    pool.sem_inc(passed["pool"], 1)
                    pool.tensor_scalar(var[:], src[:, :, 1], scale, eps, ALU.mult, ALU.add).then_inc(mid, 1)
                    pool.wait_ge(mid, b.at + 1)
                    pool.sem_inc(passed["pool"], 1)
                    pool.tensor_tensor(rstd[:], var[:], minus_half[:, 0:3], ALU.pow).then_inc(ready, 1)

                def body(m, e):
                    now = batch(m, e)
                    for j in range(JOBS):
                        if live(now):
                            p = pr[j % PSLOTS]
                            pool.wait_ge(exp_done, 2 * (JOBS * now.at + j) + 2)
                            pool.sem_inc(passed["pool"], 1)
                            two = [[0, 2], [1, P]]
                            for ap, pat in ((p[:, 0:2, 0:P], two),
                                            (p[:, 2, :].rearrange("p (a c) -> p a c", c=W1)[:, :, 0:P], two),
                                            (p[:, 0:2, W0:W0 + W2], [[0, 2], [1, W2]])):
                                pool.affine_select(out=ap, in_=ap, compare_op=ALU.is_ge, fill=0.0, base=0,
                                                   pattern=pat, channel_multiplier=-1).then_inc(causal, 1)
                        b = batch(m, e - 1)
                        if j == 3 and live(b):
                            pool.wait_ge(res_in, 32 * b.at + 32)
                            pool.sem_inc(passed["pool"], 1)
                            pool.tensor_tensor(res[:], res[:], bp[:].unsqueeze(1).broadcast_to([P, 3, D]), ALU.add).then_inc(res_ready, 1)
                        if j == 5 and live(batch(m, e + 2)):
                            power(mv, 1.0, EPS, var1, rstd1, batch(m, e + 2), mv_ready, var_ready, rstd_ready)
                        if j == 6 and live(b):
                            power(mv2, 1.0 + EPS, EPS * EPS, var2, rstd2, b, mv2_ready, var2_ready, rstd2_ready)

                power(mv, 1.0, EPS, var1, rstd1, batch(0, 0), mv_ready, var_ready, rstd_ready)
                iterations(pool, body)

            @block.scalar
            def _(act):
                act.wait_ge(dve_set, 1)
                act.wait_ge(pool_set, NEED_POOL)

                def take(name, b):
                    db = bank_of[name]
                    act.wait_ge(made[name], b.at + 1)
                    if name in ("xt0", "xt1"):
                        act.copy(xh[:, int(name[2]), :], db[:, 0:SEQ]).then_inc(xh_ready, 1)
                    elif name in ("q0", "q1"):
                        for c in (2 * int(name[1]), 2 * int(name[1]) + 1):
                            act.activation(qa[b.par][0:HR, c, :], db[HR * (c % 2):HR * (c % 2) + HR, 0:SEQ], ACT.Identity,
                                           bias=bqk[:, c:c + 1]).then_inc(qh_ready, 1)
                    elif name in ("k0", "k1"):
                        need(act, km_ready, 2 * HEADS * b.at)
                        for c in (2 * int(name[1]), 2 * int(name[1]) + 1):
                            act.activation(kh[0:HR, c, :], db[HR * (c % 2):HR * (c % 2) + HR, 0:SEQ], ACT.Identity,
                                           bias=bqk[:, 4 + c:5 + c]).then_inc(kh_ready, 1)
                    elif name in ("nm0", "nm1"):
                        c = 2 * int(name[2])
                        act.mul(qb[b.par][HR:HR + 32, c, :], db[HR:HR + 32, 0:SEQ], -1.0).then_inc(nm_half, 1)
                        act.mul(qb[b.par][HR:HR + 32, c + 1, :], db[HR + 32:P, 0:SEQ], -1.0).then_inc(taken[name], 1)
                    elif name in ("ox0", "ox1"):
                        act.copy(ont[:, int(name[2]), :], db[:, 0:SEQ]).then_inc(taken[name], 1)
                    elif name in ("zt0", "zt1"):
                        c = int(name[2])
                        act.activation(zt[:, c, :], db[:, 0:SEQ], ACT.Identity, bias=lnb[:, c:c + 1], scale=lng[:, c:c + 1],
                                       accum_out=zsum[:, c:c + 1]).then_inc(taken[name], 1)
                    elif name == "rt":
                        act.wait_ge(shifted_ready, b.at + 1)
                        act.activation(expd[:], shifted[:], ACT.Exp, accum_out=esum[:]).then_inc(esum_ready, 1)
                    elif name == "fd":
                        act.activation(hid[0:HID, :], db[0:HID, 0:SEQ], ACT.Relu, bias=bd[:]).then_inc(taken[name], 1)
                    elif name[0:2] == "pv":
                        act.copy(ot[b.par][:, int(name[2]), :], db[:, 0:SEQ]).then_inc(taken[name], 1)

                def exps(b, j):
                    p = pr[j % PSLOTS]
                    act.wait_ge(st_ready, JOBS * b.at + j + 1)
                    need(act, made[f"pv{(j - 4) % JOBS // 2}"], b.at + (1 if j >= 4 else 0))
                    act.activation(p[:, 0:2, :], st[:, 0:2, 0:W0 + W2], ACT.Exp).then_inc(exp_done, 1)
                    act.activation(p[:, 2, :], st[:, 2, 0:2 * W1], ACT.Exp).then_inc(exp_done, 1)

                def body(m, e):
                    for j in range(JOBS):
                        for item in STEPS[j]:
                            if item == "st1" and live(batch(m, e)):
                                exps(batch(m, e), j)
                            elif not isinstance(item, str) and live(batch(m, e + item[1])):
                                if item[0] in ACT_TAKES:
                                    take(item[0], batch(m, e + item[1]))

                iterations(act, body)

            @block.vector
            def _(dve):
                for q in range(2):
                    dve.memset(ka[q][:], 0.0)
                    dve.memset(kb[q][0:HR], 0.0)
                    dve.memset(qb[q][:], 0.0)
                    dve.memset(v[q][:], 0.0)
                    dve.memset(mx[q][:], 0.0)
                dve.memset(hid[HID:HID + 1, :], 1.0)
                dve.memset(h[:, 2, :], 0.0)
                dve.memset(res[:, 2, :], 0.0)
                dve.memset(h2[:, 2, :], 0.0)
                dve.memset(on[:, 2, :], 0.0).then_inc(setup_done, 1)
                dve.wait_ge(setup_done, 1)
                for q in range(2):
                    dve.memset(v[q][:, :, :, DH:DH + 1], 1.0)
                dve.wait_ge(weights_in, 13 * 16)
                dve.tensor_scalar(bqk[:, 0:4], bqk[:, 0:4], 0.25, None, ALU.mult)
                dve.tensor_scalar(wa[:, :, 0:D], wa[:, :, 0:D], 0.25, None, ALU.mult).then_inc(setup_done, 1)
                dve.wait_ge(setup_done, 2)
                dve.tensor_copy(wah[:], wa[:]).then_inc(setup_done, 1)
                dve.wait_ge(setup_done, 3)
                dve.tensor_tensor(wal[:], wa[:], wah[:], ALU.subtract).then_inc(dve_set, 1)
                dve.wait_ge(pool_set, NEED_POOL)
                dve.tensor_tensor(band2[:], band[:, 0:4], band[:, 4:8], ALU.add)
                dve.tensor_tensor(bns[:], bns[:], bng[:], ALU.mult).then_inc(setup_done, 1)
                dve.wait_ge(setup_done, 4)
                dve.tensor_tensor(bnt[:], bns[:], bnm[:], ALU.mult).then_inc(setup_done, 1)
                dve.wait_ge(setup_done, 5)
                dve.tensor_tensor(bnt[:], bnb[:], bnt[:], ALU.subtract)
                dve.tensor_scalar(bns[:], bns[:], 1.0 / SEQ, None, ALU.mult).then_inc(setup_done, 1)
                dve.wait_ge(setup_done, 6)

                def statistics(src, stat, mean_var, b, ready, done):
                    for t in range(3):
                        dve.bn_stats(stat[:, t, :], src[:, t, :]).then_inc(ready, 1)
                    dve.wait_ge(ready, 3 * b.at + 3)
                    dve.sem_inc(passed["dve"], 1)
                    for t in range(3):
                        dve.bn_aggr(mean_var[:, t, :], stat[:, t, :]).then_inc(done, 1)

                def normalise(dst, src, mean_var, rstd, b, got, done):
                    dve.wait_ge(got, b.at + 1)
                    dve.sem_inc(passed["dve"], 1)
                    for t in range(3):
                        dve.tensor_scalar(dst[:, t, :], src[:, t, :], mean_var[:, t, 0:1], rstd[:, t:t + 1],
                                          ALU.subtract, ALU.mult).then_inc(done, 1)

                def first_norm_stats(b):
                    dve.wait_ge(h_in, 32 * b.at + 32)
                    statistics(h, stats, mv, b, stats_ready, mv_ready)

                def take(name, b):
                    db = bank_of[name]
                    if name in ("xt0", "xt1"):
                        c = int(name[2])
                        dve.wait_ge(xh_ready, 2 * b.at + c + 1)
                        dve.tensor_tensor(xl[:, c, :], db[:, 0:SEQ], xh[:, c, :], ALU.subtract).then_inc(taken[name], 1)
                    elif name in ("q0", "q1"):
                        c = 2 * int(name[1])
                        dve.wait_ge(qh_ready, 4 * b.at + c + 2)
                        dve.scalar_tensor_tensor(qa[b.par][HR:P, c, :], db[0:HR, 0:SEQ], bqk[:, c:c + 1], qa[b.par][0:HR, c, :],
                                                 ALU.add, ALU.subtract)
                        dve.scalar_tensor_tensor(qa[b.par][HR:P, c + 1, :], db[HR:P, 0:SEQ], bqk[:, c + 1:c + 2],
                                                 qa[b.par][0:HR, c + 1, :], ALU.add, ALU.subtract).then_inc(taken[name], 1)
                    elif name in ("k0", "k1"):
                        c = 2 * int(name[1])
                        dve.wait_ge(kh_ready, 4 * b.at + c + 2)
                        dve.scalar_tensor_tensor(kl[:, c, :], db[0:HR, 0:SEQ], bqk[:, 4 + c:5 + c], kh[0:HR, c, :],
                                                 ALU.add, ALU.subtract)
                        dve.scalar_tensor_tensor(kl[:, c + 1, :], db[HR:P, 0:SEQ], bqk[:, 5 + c:6 + c], kh[0:HR, c + 1, :],
                                                 ALU.add, ALU.subtract).then_inc(taken[name], 1)
                    elif name == "v01":
                        dve.wait_ge(made[name], b.at + 1)
                        dve.tensor_tensor(v[b.par][:, 0:2, :, 0:DH], db[:].rearrange("p (t h d) -> p t h d", t=2, d=DH),
                                          bv[:].unsqueeze(1).broadcast_to([P, 2, HEADS, DH]), ALU.add).then_inc(taken[name], 1)
                    elif name == "v2":
                        dve.wait_ge(made[name], b.at + 1)
                        dve.tensor_tensor(v[b.par][0:TXT, 2, :, 0:DH], db[0:TXT, 0:D].rearrange("p (h d) -> p h d", d=DH),
                                          bv[0:TXT], ALU.add).then_inc(taken[name], 1)
                    elif name in ("ot0", "ot1", "ot2"):
                        t = int(name[2])
                        n = TXT if t == 2 else P
                        o = db[0:n, :].rearrange("p (h d) -> p h d", d=2 * DH)
                        dve.wait_ge(made[name], b.at + 1)
                        dve.reciprocal(rden[0:n, t, :], o[:, :, DH]).then_inc(rden_ready, 1)
                        dve.wait_ge(rden_ready, 3 * b.at + t + 1)
                        dve.tensor_tensor(on[0:n, t, :].rearrange("p (h d) -> p h d", d=DH), o[:, :, 0:DH],
                                          rden[0:n, t, :].unsqueeze(2).broadcast_to([n, HEADS, DH]), ALU.mult).then_inc(taken[name], 1)
                    elif name == "pr01":
                        dve.wait_ge(res_ready, b.at + 1)
                        dve.wait_ge(made[name], b.at + 1)
                        dve.tensor_tensor(h2[:, 0:2, :], db[:].rearrange("p (t n) -> p t n", t=2), res[:, 0:2, :],
                                          ALU.add).then_inc(taken[name], 1)
                    elif name == "pr2":
                        dve.wait_ge(made[name], b.at + 1)
                        dve.tensor_tensor(h2[0:TXT, 2, :], db[0:TXT, 0:D], res[0:TXT, 2, :], ALU.add).then_inc(taken[name], 1)
                        dve.wait_ge(taken["pr01"], b.at + 1)
                        dve.wait_ge(taken["pr2"], b.at + 1)
                        statistics(h2, stats2, mv2, b, stats2_ready, mv2_ready)
                    elif name == "rt":
                        dve.wait_ge(made[name], b.at + 1)
                        dve.tensor_tensor(logit[:], db[:, 0:EXPERTS], brt[:], ALU.add).then_inc(taken[name], 1)
                        dve.wait_ge(taken[name], b.at + 1)
                        dve.sem_inc(passed["dve"], 1)
                        dve.max(top[:], logit[:]).then_inc(top_ready, 1)
                        dve.wait_ge(top_ready, b.at + 1)
                        dve.sem_inc(passed["dve"], 1)
                        dve.max_index(topi[:], top[:], logit[:]).then_inc(topi_ready, 1)
                        dve.tensor_scalar(shifted[:], logit[:], top[:, 0:1], None, ALU.subtract).then_inc(shifted_ready, 1)
                    elif name == "fu01":
                        dve.wait_ge(made[name], b.at + 1)
                        need(dve, stored, 32 * b.at)
                        dve.scalar_tensor_tensor(ob[:, 0:2, :], db[:].rearrange("p (t n) -> p t n", t=2), gate[:], h2[:, 0:2, :],
                                                 ALU.mult, ALU.add).then_inc(taken[name], 1)
                    elif name == "fu2":
                        dve.wait_ge(made[name], b.at + 1)
                        dve.scalar_tensor_tensor(ob[0:TXT, 2, :], db[0:TXT, 0:D], gate[0:TXT], h2[0:TXT, 2, :],
                                                 ALU.mult, ALU.add).then_inc(taken[name], 1)

                def keys_of_head(b, hd):
                    c, r = hd // 4, hd % 4
                    if hd % 8 == 0:
                        dve.wait_ge(taken[f"k{hd // 8}"], b.at + 1)
                        dve.wait_ge(kh_twice[hd // 8], 16 * b.at + 16)
                    dve.tensor_scalar(ka[b.par][:, hd, 0:SEQ], kh[:, c, :], band2[:, r:r + 1], None, ALU.mult).then_inc(km_ready, 1)
                    dve.tensor_scalar(kb[b.par][0:HR, hd, 0:SEQ], kl[:, c, :], band2[0:HR, r:r + 1], None,
                                      ALU.mult).then_inc(km_ready, 1)

                def maxima(m, e, j):
                    b, jb = score_job(m, e, j)
                    if not live(b):
                        return
                    c = HR + 32 * (jb % 4 // 2) + 2 * (jb % 2)
                    rows = mx[jb // 4]
                    dve.wait_ge(sc_ready, JOBS * b.at + jb + 1)
                    dve.reduce_max(rows[:, 2, c:c + 2], sc[:, 0:2, 0:W0], AX.X).then_inc(mx_ready, 1)
                    dve.reduce_max(rows[0:TXT, 0, c:c + 2], sc[0:TXT, 0:2, W0:W0 + W2], AX.X).then_inc(mx_ready, 1)
                    dve.reduce_max(rows[:, 1, c:c + 2], sc[:, 2, 0:2 * W1].rearrange("p (a c) -> p a c", a=2),
                                   AX.X).then_inc(mx_ready, 1)

                spread = {2: (0,), 3: (1,), 4: (2, 3), 5: (4,), 6: (5,), 7: (6, 7)}

                def body(m, e):
                    for j in range(JOBS):
                        for item in STEPS[j]:
                            if item == "sc":
                                maxima(m, e, j)
                            elif not isinstance(item, str) and live(batch(m, e + item[1])):
                                take(item[0], batch(m, e + item[1]))
                        b = batch(m, e + 1)
                        if live(b):
                            for pair in spread.get(j, ()):
                                keys_of_head(b, 2 * pair)
                                keys_of_head(b, 2 * pair + 1)
                        b = batch(m, e - 2)
                        if j == 1 and live(b):
                            dve.wait_ge(esum_ready, b.at + 1)
                            dve.reciprocal(gate[:], esum[:]).then_inc(gate_ready, 1)
                        if j == 2 and live(b):
                            dve.wait_ge(gate_ready, b.at + 1)
                            dve.sem_inc(passed["dve"], 1)
                        b = batch(m, e + 2)
                        if j == 4 and live(b):
                            first_norm_stats(b)
                        if j == 6 and live(b):
                            normalise(xn, h, mv, rstd1, b, rstd_ready, xn_ready)
                        b = batch(m, e - 1)
                        if j == 6 and live(b):
                            normalise(zn, h2, mv2, rstd2, b, rstd2_ready, zn_ready)
                        if j == 7 and live(b):
                            dve.wait_ge(taken["zt1"], b.at + 1)
                            dve.tensor_tensor(zb[:], zsum[:], bns[:], ALU.mult).then_inc(zb_mul, 1)
                            dve.wait_ge(zb_mul, b.at + 1)
                            dve.tensor_tensor(zb[:], zb[:], bnt[:], ALU.add).then_inc(zb_ready, 1)

                first_norm_stats(batch(0, 0))
                normalise(xn, h, mv, rstd1, batch(0, 0), rstd_ready, xn_ready)
                iterations(dve, body)

            @block.tensor
            def _(pe):
                pe.wait_ge(pool_set, NEED_POOL)
                pe.wait_ge(dve_set, 1)

                def tile(t):
                    return slice(P * t, min(P * t + P, SEQ))

                def make(name, b, before):
                    db = bank_of[name]
                    if before is not None:
                        pe.wait_ge(taken[before[0]], before[1].at + 1)
                    if name in ("xt0", "xt1"):
                        c = int(name[2])
                        pe.wait_ge(xn_ready, 3 * b.at + 3)
                        for t in range(3):
                            ins = pe.transpose(db[:, P * t:P * t + P], xn[:, t, P * c:P * c + P], ident[:])
                    elif name in ("q0", "q1", "k0", "k1"):
                        col = (D if name[0] == "k" else 0) + P * int(name[1])
                        pe.wait_ge(taken["xt1"], b.at + 1)
                        for c in range(CD):
                            for n, (w, x) in enumerate(((wah, xh), (wah, xl), (wal, xh))):
                                ins = pe.matmul(db[:, 0:SEQ], w[:, c, col:col + P], x[:, c, :],
                                                start=c + n == 0, stop=c * n == 2)
                    elif name in ("v01", "v2"):
                        for n, t in enumerate((0, 1) if name == "v01" else (2,)):
                            k = tile(t)
                            for c in range(CD):
                                for i, (x, w) in enumerate(((xh, wah), (xh, wal), (xl, wah))):
                                    ins = pe.matmul(db[0:k.stop - k.start, D * n:D * n + D], x[:, c, k], w[:, c, 2 * D:3 * D],
                                                    start=c + i == 0, stop=c * i == 2)
                    elif name in ("nm0", "nm1"):
                        u = int(name[2])
                        pe.wait_ge(mx_ready, 3 * (JOBS * b.at + 4 * u + 4))
                        for t, (q0, q1) in enumerate(QT):
                            n = q1 - q0
                            ins = pe.transpose(db[:, q0:q1], mx[u][0:n, t, :], ident[0:n, 0:n])
                    elif name in ("ot0", "ot1", "ot2"):
                        k = tile(int(name[2]))
                        pe.wait_ge(taken["pv3"], b.at + 1)
                        for g in range(4):
                            ins = pe.transpose(db[0:k.stop - k.start, P * g:P * g + P], ot[b.par][:, g, k], ident[:])
                    elif name in ("ox0", "ox1"):
                        c = int(name[2])
                        for t in range(3):
                            k = tile(t)
                            n = k.stop - k.start
                            ins = pe.transpose(db[:, k], on[0:n, t, P * c:P * c + P], ident[0:n, 0:n])
                    elif name in ("pr01", "pr2"):
                        pe.wait_ge(taken["ox1"], b.at + 1)
                        for n, t in enumerate((0, 1) if name == "pr01" else (2,)):
                            k = tile(t)
                            for c in range(CD):
                                ins = pe.matmul(db[0:k.stop - k.start, D * n:D * n + D], ont[:, c, k], wp[:, c, :],
                                                start=c == 0, stop=c == CD - 1)
                    elif name in ("zt0", "zt1"):
                        c = int(name[2])
                        pe.wait_ge(zn_ready, 3 * b.at + 3)
                        for t in range(3):
                            k = tile(t)
                            n = k.stop - k.start
                            ins = pe.transpose(db[:, k], zn[0:n, t, P * c:P * c + P], ident[0:n, 0:n])
                    elif name == "rt":
                        pe.wait_ge(zb_ready, b.at + 1)
                        for c in range(CD):
                            ins = pe.matmul(db[:, 0:EXPERTS], zb[:, c:c + 1].broadcast_to([P, P]), wrt[:, c, :],
                                            start=c == 0, stop=c == CD - 1)
                    elif name == "fd":
                        pe.wait_ge(expert_in, 64 * b.at + 64)
                        pe.wait_ge(taken["zt1"], b.at + 1)
                        for c in range(CD):
                            ins = pe.matmul(db[0:HID, 0:SEQ], wd[:, c, :], zt[:, c, :], start=c == 0, stop=c == CD - 1)
                    elif name in ("fu01", "fu2"):
                        for n, t in enumerate((0, 1) if name == "fu01" else (2,)):
                            k = tile(t)
                            ins = pe.matmul(db[0:k.stop - k.start, D * n:D * n + D], hid[:, k], wu[:], start=True, stop=True)
                    elif name[0:2] == "pv":
                        g = int(name[2])
                        if g == 0:
                            pe.wait_ge(taken["v2"], b.at + 1)
                        pe.wait_ge(causal, 3 * (JOBS * b.at + 2 * g + 2))
                        pe.sem_inc(passed["pe"], 1)
                        for n, (_, q0) in enumerate(KT):
                            for a in range(4):
                                p = pr[(2 * g + a // 2) % PSLOTS]
                                aa = a % 2
                                src = (p[:, aa, 0:W0], p[:, 2, W1 * aa:W1 * aa + W1], p[:, aa, W0:W0 + W2])[n]
                                ins = pe.matmul(db[32 * a:32 * a + 32, q0:SEQ], v[b.par][:, n, 4 * g + a, :], src,
                                                start=n == 0, stop=n == 2)
                    ins.then_inc(made[name], 1)

                def scores_t(b, j, a):
                    hd = 2 * j + a
                    c = hd // 4
                    if a == 0:
                        if j % 4 == 0:
                            pe.wait_ge(taken[f"nm{j // 4}"], b.at + 1)
                            pe.wait_ge(qh_twice, 16 * b.at + 16)
                        need(pe, exp_done, 2 * (JOBS * b.at + j))
                    for (k0, q0), o in zip(KT, (st[:, a, 0:W0], st[:, 2, W1 * a:W1 * a + W1], st[:, a, W0:W0 + W2])):
                        pe.matmul(o, ka[b.par][:, hd, k0:k0 + P], qa[b.par][:, c, q0:SEQ], start=True, stop=False)
                        ins = pe.matmul(o, kb[b.par][:, hd, k0:k0 + P], qb[b.par][:, c, q0:SEQ], start=False, stop=True)
                    if a == 1:
                        ins.then_inc(st_ready, 1)

                def scores(b, j):
                    pe.wait_ge(km_ready, 2 * HEADS * b.at + 4 * j + 4)
                    need(pe, mx_ready, 3 * (JOBS * b.at + j))
                    for a in range(2):
                        hd = 2 * j + a
                        for (q0, q1), o in zip(QT, (sc[0:TXT, a, W0:W0 + W2], sc[:, 2, W1 * a:W1 * a + W1], sc[:, a, 0:W0])):
                            n = q1 - q0
                            pe.matmul(o[:, q0:q1], ident16[:, 0:n], later[:, 0:n], start=True, stop=False, skip_group_check=True)
                            ins = pe.matmul(o, qa[b.par][:, hd // 4, q0:q1], ka[b.par][:, hd, 0:q1],
                                            start=False, stop=True, skip_group_check=True)
                    ins.then_inc(sc_ready, 1)

                def body(m, e):
                    now = batch(m, e)
                    for j in range(JOBS):
                        for item in STEPS[j]:
                            if item == "sc":
                                b, jb = score_job(m, e, j)
                                if live(b):
                                    scores(b, jb)
                            elif isinstance(item, str):
                                if live(now):
                                    scores_t(now, j, int(item[2]))
                            elif live(batch(m, e + item[1])):
                                make(item[0], batch(m, e + item[1]), slice_before(m, e, item[0]))

                iterations(pe, body)


_INS = ['x', 'txt', 'L0_tok_log_dt', 'L0_tok_inv_A_real', 'L0_tok_A_imag', 'L0_tok_B_ri', 'L0_attn_w_attn',
        'L0_attn_b_attn', 'L0_attn_w_proj', 'L0_attn_b_proj', 'L0_ffn_ln_g', 'L0_ffn_ln_b', 'L0_ffn_bn_g',
        'L0_ffn_bn_b', 'L0_ffn_bn_mean', 'L0_ffn_bn_var', 'L0_ffn_Wr', 'L0_ffn_br', 'L0_ffn_W_down',
        'L0_ffn_b_down', 'L0_ffn_W_up', 'L0_ffn_b_up']


def kernel(**inputs):
    import numpy as _np
    import concourse.bacc as _bacc
    from concourse import mybir as _mybir
    from concourse.bass_utils import run_bass_kernel_spmd as _run

    nc = _bacc.Bacc("TRN2", target_bir_lowering=False, num_devices=1)
    arrays, args = {}, []
    for name in _INS:
        a = _np.ascontiguousarray(inputs[name])
        arrays[f"in_{name}_dram"] = a
        args.append(nc.dram_tensor(f"in_{name}_dram", a.shape, _mybir.dt.from_np(a.dtype), kind="ExternalInput").ap())
    out = nc.dram_tensor("out_0_dram", (32, 333, 256), _mybir.dt.float32, kind="ExternalOutput").ap()
    scratch = nc.dram_tensor("token_scratch", (32, 256, 256), _mybir.dt.float32, kind="Internal").ap()
    x, txt, log_dt, inv_a, a_imag, b_ri = args[:6]
    build_tokens(nc, x, log_dt, inv_a, a_imag, b_ri, scratch)
    build_layer(nc, scratch, txt, *args[6:], out)
    r = _run(nc, [arrays], core_ids=[0])
    return r.results[0]["out_0_dram"]
```

```python
import concourse.bass as bass
from concourse import mybir
from collections import namedtuple
from contextlib import ExitStack

F32 = mybir.dt.float32
F16 = mybir.dt.float16
BF16 = mybir.dt.bfloat16
U32 = mybir.dt.uint32
ALU = mybir.AluOpType
ACT = mybir.ActivationFunctionType
AX = mybir.AxisListType

P = 128
BATCH, HK, NS, D = 32, 256, 64, 256
TXT = 77
SEQ = HK + TXT
SEQP = 3 * P
HEADS, DH = 16, 16
EXPERTS, HID = 8, 64
EPS = 1e-5
CD = D // P
HR = 2 * DH
R3 = 3 * HR
MASKED = -30000.0
EULER = 2.718281828459045

HP = HK // 2
HPC = 16
CHUNKS = HP // HPC
LV = 128
SQUARINGS = 7

QT = [(0, TXT), (TXT, TXT + P), (TXT + P, SEQ)]
KT = [(0, 0), (P, P), (2 * P, 2 * P)]
W0, W1, W2 = SEQ, SEQ - P, SEQ - 2 * P


def build_tokens(nc, x, log_dt, inv_a, a_imag, b_ri, scratch, layer, weights):
    x_v = x.rearrange("c (h q) n r -> c h (q n r)", q=2)
    scr_v = scratch.rearrange("c (h q) l -> q c h l", q=2)
    ctx = ExitStack()
    with ctx:
        def sb(name, shape, dt=F32):
            return ctx.enter_context(nc.sbuf_tensor(name, shape, dt))

        def sem(name):
            return ctx.enter_context(nc.semaphore(name))

        ident = sb("ident1", [P, P])
        ld = sb("ld", [P, 2])
        ia = sb("ia", [P, 2, NS])
        ai = sb("ai", [P, 2, NS])
        braw = sb("braw", [P, 2, NS, 2])
        euler = sb("euler", [P, 2])
        dt = sb("dt", [P, 2])
        decay = sb("decay", [P, 2, NS])
        wr = sb("wr", [P, 2, NS])
        wi = sb("wi", [P, 2, NS])
        sq = sb("sq", [P, 2, NS])
        den = sb("den", [P, 2, NS])
        pre = sb("pre", [P, 4, 2, NS])
        bt = sb("bt", [P, 2, HP])
        zr = sb("zr", [P, SQUARINGS + 1, HP])
        zi = sb("zi", [P, SQUARINGS + 1, HP])
        nzi = sb("nzi", [P, SQUARINGS + 1, HP])
        dif = sb("dif", [P, HP])
        tot = sb("tot", [P, HP])
        xin = [sb(f"xin{q}", [P, 4, 4 * NS]) for q in range(2)]
        a = [sb(f"c{q}", [P, 2, HPC, 2, 2, BATCH]) for q in range(2)]
        a0 = [sb(f"c_dense{q}", [P, 2, HPC, BATCH]) for q in range(2)]
        a1 = sb("c_turned", [P, 2, HPC, BATCH])
        v = [sb(f"powers{q}", [P, 2, HPC, LV]) for q in range(2)]
        vtmp = sb("vtmp", [P, 2, HPC, LV // 2])
        atmp = sb("atmp", [P, 2, HPC, BATCH])
        hst = [sb(f"hst{q}", [P, HPC, LV]) for q in range(2)]
        tp = ctx.enter_context(nc.psum_tensor("tp", [P, 2, 512], F32))
        kp = [ctx.enter_context(nc.psum_tensor(f"kp{q}", [P, 4, LV], F32)) for q in range(4)]

        par_in = sem("par_in")
        ident_set = sem("ident_set")
        euler_set = sem("euler_set")
        pow_done = sem("pow_done")
        link = sem("param_link")
        pre_ready = sem("pre_ready")
        pre_t = sem("pre_transposed")
        bt_ready = sem("bt_ready")
        z_link = sem("z_link")
        z_ready = sem("z_ready")
        xin_in = [sem(f"xin_in{q}") for q in range(2)]
        ct_ready = sem("ct_ready")
        a0_ready = sem("a0_ready")
        c_ready = sem("c_ready")
        zeros_set = sem("zeros_set")
        a1_mul = sem("a1_mul")
        a1_ready = sem("a1_ready")
        v_link = sem("v_link")
        v_ready = sem("v_ready")
        k_ready = sem("k_ready")
        k_taken = sem("k_taken")
        hst_out = [sem(f"hst_out{q}") for q in range(2)]
        pool_passed = sem("pool_passed1")
        sp_passed = sem("sp_passed1")
        pe_passed = sem("pe_passed1")

        LINKS = 1 + 4 * SQUARINGS

        def chunks(eng, body):
            body(0, 0, 0)
            body(1, 0, 1)
            with eng.Fori(1, CHUNKS // 2 - 1) as m:
                body(2 * m, m, 0)
                body(2 * m + 1, m, 1)
            body(CHUNKS - 2, CHUNKS // 2 - 1, 0)
            body(CHUNKS - 1, CHUNKS // 2 - 1, 1)

        def first(k):
            return isinstance(k, int) and k < 2

        def last(k):
            return isinstance(k, int) and k == CHUNKS - 1

        with nc.Block() as block:

            @block.sync
            def _(sp):
                sp.dma_start(ld[:], log_dt.rearrange("(h q) -> h q", q=2)).then_inc(par_in, 16)
                sp.dma_start(ia[:], inv_a.rearrange("(h q) n -> h q n", q=2)).then_inc(par_in, 16)
                sp.dma_start(ai[:], a_imag.rearrange("(h q) n -> h q n", q=2)).then_inc(par_in, 16)
                sp.dma_start(braw[:], b_ri.rearrange("(h q) n r -> h q n r", q=2)).then_inc(par_in, 16)

                def load(k, q):
                    for t in range(4):
                        sp.dma_start(xin[q][:, t, :], x_v[8 * t:8 * t + 8, bass.ds(HPC * k, HPC), :]).then_inc(xin_in[q], 16)

                load(0, 0)
                load(1, 1)
                load_constants(sp, layer, *weights)

                def body(k, m, q):
                    if not (isinstance(k, int) and k == 0) and not last(k):
                        sp.wait_ge(ct_ready, k)
                        sp.sem_inc(sp_passed, 1)
                        load(k + 1, 1 - q)
                    if not (isinstance(k, int) and k == 0):
                        store(k - 1, 1 - q)

                def store(k, q):
                    sp.wait_ge(k_taken, 4 * k + 4)
                    sp.sem_inc(sp_passed, 1)
                    for par in range(2):
                        for i in range(2):
                            p0 = 64 * par + 32 * i
                            sp.dma_start(scr_v[par, :, bass.ds(HPC * k, HPC), i * LV:(i + 1) * LV],
                                         hst[q][p0:p0 + 32, :, :]).then_inc(hst_out[q], 16)

                chunks(sp, body)
                store(CHUNKS - 1, 1)
                for q in range(2):
                    sp.wait_ge(hst_out[q], 64 * (CHUNKS // 2))
                sp.wait_ge(layer.weights_in, 13 * 16)

            @block.gpsimd
            def _(pool):
                pool.memset(ident[:], 0.0).then_inc(ident_set, 1)
                pool.memset(euler[:], EULER).then_inc(euler_set, 1)
                pool.wait_ge(ident_set, 1)
                pool.affine_select(out=ident[:], in_=ident[:], compare_op=ALU.not_equal, fill=1.0, base=0,
                                   pattern=[[-1, P]], channel_multiplier=1).then_inc(ident_set, 1)
                pool.wait_ge(euler_set, 1)
                pool.wait_ge(par_in, 64)
                pool.tensor_tensor(dt[:], euler[:], ld[:], ALU.pow).then_inc(pow_done, 1)
                for q in range(2):
                    pool.memset(a[q][:], 0.0).then_inc(zeros_set, 1)
                fill_constants(pool, layer)

                def body(k, m, q):
                    if isinstance(k, int) and k == 0:
                        pool.wait_ge(z_ready, 1)
                    pool.wait_ge(a0_ready, 2 * k + 2)
                    if isinstance(k, int) and k == 0:
                        pool.wait_ge(zeros_set, 2)
                    hs = bass.ds(HPC * k, HPC)

                    def zb(z):
                        return z[:, SQUARINGS, hs].unsqueeze(2).broadcast_to([P, HPC, BATCH])

                    src = a0[q]
                    pool.tensor_tensor(a1[:, 0], src[:, 0], zb(zr), ALU.mult).then_inc(a1_mul, 1)
                    pool.tensor_tensor(a1[:, 1], src[:, 1], zb(zr), ALU.mult).then_inc(a1_mul, 1)
                    pool.tensor_tensor(atmp[:, 0], src[:, 1], zb(zi), ALU.mult).then_inc(a1_mul, 1)
                    pool.tensor_tensor(atmp[:, 1], src[:, 0], zb(nzi), ALU.mult).then_inc(a1_mul, 1)
                    pool.wait_ge(a1_mul, 4 * k + 4)
                    for par in range(2):
                        rows = slice(64 * par, 64 * par + 64)
                        pool.tensor_tensor(a[q][rows, :, :, par, 1, :], a1[rows], atmp[rows], ALU.add).then_inc(a1_ready, 1)
                        pool.wait_ge(a1_ready, 2 * k + 1 + par)

                chunks(pool, body)

            @block.scalar
            def _(act):
                act.wait_ge(par_in, 64)
                act.activation(decay[:], ia[:], ACT.Exp).then_inc(pow_done, 1)
                act.wait_ge(z_link, 2)
                act.copy(bt[:, :, :], tp[:, 0, 256:512].rearrange("p (r h) -> p r h", r=2)).then_inc(bt_ready, 1)

                def take_c(k, q):
                    act.wait_ge(ct_ready, k + 1)
                    if not first(k):
                        act.wait_ge(a1_ready, 2 * k - 2)
                    for ri in range(2):
                        act.mul(a0[q][:, ri, :, :].rearrange("p h c -> p c h"),
                                tp[:, ri, :].rearrange("p (c h) -> p c h", h=HPC),
                                1.0 - 2.0 * ri).then_inc(a0_ready, 1)
                    if not first(k):
                        act.wait_ge(k_ready, 4 * k - 4)
                    act.wait_ge(a0_ready, 2 * k + 2)
                    for par in range(2):
                        rows = slice(64 * par, 64 * par + 64)
                        act.copy(a[q][rows, :, :, par, 0, :], a0[q][rows]).then_inc(c_ready, 1)

                act.wait_ge(zeros_set, 2)
                take_c(0, 0)

                def body(k, m, q):
                    if not last(k):
                        take_c(k + 1, 1 - q)
                    if not first(k):
                        act.wait_ge(hst_out[q], 64 * m)
                    for g in range(4):
                        act.wait_ge(k_ready, 4 * k + g + 1)
                        act.copy(hst[q][:, 4 * g:4 * g + 4, :], kp[g][:]).then_inc(k_taken, 1)

                chunks(act, body)

            @block.vector
            def _(dve):
                n = [0]

                def step(ins):
                    n[0] += 1
                    ins.then_inc(link, 1)

                def done():
                    dve.wait_ge(link, n[0])

                dve.wait_ge(pow_done, 2)
                dve.wait_ge(par_in, 64)
                dtb = dt[:].unsqueeze(2).broadcast_to([P, 2, NS])
                step(dve.scalar_tensor_tensor(wr[:], decay[:], -0.5, dtb, ALU.mult, ALU.mult))
                step(dve.scalar_tensor_tensor(wi[:], ai[:], 0.5, dtb, ALU.mult, ALU.mult))
                done()
                step(dve.tensor_scalar(sq[:], wr[:], -1.0, 1.0, ALU.mult, ALU.add))
                step(dve.tensor_tensor(tot[:].rearrange("p (q n) -> p q n", q=2), wi[:], wi[:], ALU.mult))
                done()
                wi2 = tot[:].rearrange("p (q n) -> p q n", q=2)
                step(dve.tensor_tensor(den[:], sq[:], sq[:], ALU.mult))
                step(dve.scalar_tensor_tensor(pre[:, 0], wr[:], 1.0, sq[:], ALU.add, ALU.mult))
                done()
                step(dve.tensor_tensor(den[:], den[:], wi2, ALU.add))
                step(dve.tensor_tensor(pre[:, 0], pre[:, 0], wi2, ALU.subtract))
                done()
                step(dve.reciprocal(den[:], den[:]))
                done()
                dve.tensor_tensor(pre[:, 0], pre[:, 0], den[:], ALU.mult).then_inc(pre_ready, 1)
                dve.scalar_tensor_tensor(pre[:, 1], wi[:], 2.0, den[:], ALU.mult, ALU.mult).then_inc(pre_ready, 1)
                dve.tensor_scalar(pre[:, 2], braw[:, :, :, 0], 2.0, None, ALU.mult).then_inc(pre_ready, 1)
                dve.tensor_scalar(pre[:, 3], braw[:, :, :, 1], 2.0, None, ALU.mult).then_inc(pre_ready, 1)
                dve.wait_ge(pre_t, 1)
                c = 0

                def zstep(ins):
                    ins.then_inc(z_link, 1)

                zstep(dve.tensor_copy(zr[:, 0, :], tp[:, 0, 0:P]))
                zstep(dve.tensor_copy(zi[:, 0, :], tp[:, 0, P:2 * P]))
                c += 2
                for k in range(SQUARINGS):
                    dve.wait_ge(z_link, c)
                    zstep(dve.tensor_tensor(dif[:], zr[:, k], zi[:, k], ALU.subtract))
                    zstep(dve.tensor_tensor(tot[:], zr[:, k], zi[:, k], ALU.add))
                    zstep(dve.scalar_tensor_tensor(zi[:, k + 1], zr[:, k], 2.0, zi[:, k], ALU.mult, ALU.mult))
                    c += 3
                    dve.wait_ge(z_link, c)
                    zstep(dve.tensor_tensor(zr[:, k + 1], dif[:], tot[:], ALU.mult))
                    c += 1
                dve.wait_ge(z_link, c)
                zstep(dve.tensor_scalar(nzi[:], zi[:], -1.0, None, ALU.mult))
                c += 1
                dve.wait_ge(z_link, c)
                dve.tensor_copy(dif[:, 0:1], dt[:, 0:1]).then_inc(z_ready, 1)

                def body(k, m, q):
                    hs = bass.ds(HPC * k, HPC)
                    base = LINKS * k
                    if isinstance(k, int) and k == 0:
                        dve.wait_ge(bt_ready, 1)
                    if not first(k):
                        dve.wait_ge(k_ready, 4 * k - 4)
                    dve.tensor_copy(v[q][:, :, :, 0:1], bt[:, :, hs].unsqueeze(3)).then_inc(v_link, 1)
                    c = 1
                    for s in range(SQUARINGS):
                        w = 1 << s

                        def zb(z):
                            return z[:, s, hs].unsqueeze(2).broadcast_to([P, HPC, w])

                        lo = v[q][:, :, :, 0:w]
                        hi = v[q][:, :, :, w:2 * w]
                        tmp = vtmp[:, :, :, 0:w]
                        dve.wait_ge(v_link, base + c)
                        dve.tensor_tensor(tmp[:, 0], lo[:, 1], zb(nzi), ALU.mult).then_inc(v_link, 1)
                        dve.tensor_tensor(tmp[:, 1], lo[:, 0], zb(zi), ALU.mult).then_inc(v_link, 1)
                        dve.tensor_tensor(hi, lo, z_both(s, hs, w), ALU.mult).then_inc(v_link, 1)
                        c += 3
                        dve.wait_ge(v_link, base + c)
                        ins = dve.tensor_tensor(hi, hi, tmp, ALU.add)
                        c += 1
                        if s == SQUARINGS - 1:
                            ins.then_inc(v_ready, 1)
                            dve.sem_inc(v_link, 1)
                        else:
                            ins.then_inc(v_link, 1)

                def z_both(s, hs, w):
                    return zr[:, s, hs].unsqueeze(1).unsqueeze(3).broadcast_to([P, 2, HPC, w])

                chunks(dve, body)
                prepare_constants(dve, layer)

            @block.tensor
            def _(pe):
                pe.wait_ge(ident_set, 2)
                pe.wait_ge(pre_ready, 4)
                for j in range(4):
                    ins = pe.transpose(tp[:, 0, P * j:P * j + P], pre[:, j].rearrange("p q n -> p (q n)"), ident[:])
                ins.then_inc(pre_t, 1)
                pe.wait_ge(bt_ready, 1)
                pe.wait_ge(z_link, 2)

                def turn_c(k, m, q):
                    pe.wait_ge(xin_in[q], 64 * m + 64)
                    if not (isinstance(k, int) and k == 0):
                        pe.wait_ge(a0_ready, 2 * k)
                    for ri in range(2):
                        for t in range(4):
                            src = xin[q][:, t, :].rearrange("p (f r) -> p r f", r=2)[:, ri, :]
                            ins = pe.transpose(tp[:, ri, P * t:P * t + P], src, ident[:])
                    ins.then_inc(ct_ready, 1)

                turn_c(0, 0, 0)

                def body(k, m, q):
                    if not last(k):
                        turn_c(k + 1, m if q == 0 else m + 1, 1 - q)
                    pe.wait_ge(v_ready, k + 1)
                    pe.wait_ge(c_ready, 2 * k + 2)
                    pe.wait_ge(a1_ready, 2 * k + 2)
                    for g in range(4):
                        if not (isinstance(k, int) and k == 0):
                            pe.wait_ge(k_taken, 4 * k + g - 3)
                        pe.sem_inc(pe_passed, 1)
                        for h in range(4 * g, 4 * g + 4):
                            for ri in range(2):
                                ins = pe.matmul(kp[g][:, h % 4, :], a[q][:, ri, h].rearrange("p r i c -> p (r i c)"),
                                                v[q][:, ri, h, :], start=ri == 0, stop=ri == 1)
                        ins.then_inc(k_ready, 1)

                chunks(pe, body)


STEPS = [
    ["st0", "sc", "st1", ("pv3", -1, 0), ("v01", 1, 1)],
    ["st0", ("ot0", -1, 0), "st1", ("ot1", -1, 1), "sc", ("ot2", -1, 0), ("v2", 1, 1)],
    ["st0", "st1", "sc", ("ox0", -1, 0), ("ox1", -1, 1), ("pv0", 0, 0), ("fd", -2, 1)],
    ["st0", "st1", ("nm1", 0, 0), "sc", ("pr01", -1, 1), ("pr2", -1, 0), ("xt0", 2, 1)],
    ["st0", ("pv1", 0, 0), "st1", "sc", ("xt1", 2, 0), ("fu01", -2, 1)],
    [("q0", 2, 0), "st0", "st1", ("k0", 2, 1), ("k1", 2, 0), "sc", ("zt0", -1, 0)],
    ["st0", "st1", ("fu2", -2, 1), "sc", ("pv2", 0, 1), ("zt1", -1, 0)],
    ["st0", ("nm0", 1, 1), ("q1", 2, 0), "st1", "sc", ("rt", -1, 1)],
]
WHEN = {"statistics": 1, "power 1": 2, "add bias": 1, "normalise 1": 2, "power 2": 3, "normalise 2": 4, "router input": 6}
SLICES = [x for step in STEPS for x in step if not isinstance(x, str)]
Q_DMAS = 13 * 16
K_DMAS = 12 * 16
ACT_TAKES = ("xt0", "xt1", "q0", "q1", "k0", "k1", "nm0", "nm1", "ox0", "ox1", "zt0", "zt1", "rt", "fd",
             "pv0", "pv1", "pv2", "pv3")
JOBS = 8
PSLOTS = 4
Batch = namedtuple("Batch", "at half par")


def batch(m, e):
    return Batch(2 * m + e, m + e // 2, e % 2)


def live(b):
    return not isinstance(b.at, int) or 0 <= b.at < BATCH


def iterations(eng, body):
    for i in range(-2, 3):
        body(0, i)
    with eng.Fori(1, BATCH // 2 - 2) as m:
        body(m, 1)
        body(m, 2)
    for i in range(BATCH - 3, BATCH + 2):
        body(0, i)


def need(eng, sem, count):
    if not isinstance(count, int) or count > 0:
        eng.wait_ge(sem, count)


def score_job(m, e, j):
    return (batch(m, e + 1), j - 3) if j >= 3 else (batch(m, e), j + 5)


def slice_before(m, e, name):
    k = [x[0] for x in SLICES].index(name)
    bank = SLICES[k][2]
    while True:
        k -= 1
        if k < 0:
            k += len(SLICES)
            e -= 1
        if e < -2 and isinstance(m, int):
            return None
        other, d, its = SLICES[k]
        if its == bank and live(batch(m, e + d)):
            return other, batch(m, e + d)


Constants = namedtuple("Constants",
                       "band band2 bnb bng bnm bns bnt bnv bp bqk brt bv ident ident16 km later lnb lng "
                       "minus_half mx ones qm v wa wah wal wp wrt zero weights_in pool_set dve_set setup_done "
                       "ones_placed ")
NEED_POOL = 14


def layer_constants(nc, ctx):
    def sb(name, shape, dt=F32):
        return ctx.enter_context(nc.sbuf_tensor(name, shape, dt))

    def sem(name):
        return ctx.enter_context(nc.semaphore(name))

    ident = sb("ident", [P, P])
    ident16 = sb("ident16", [P, P], BF16)
    later = sb("later", [P, P], BF16)
    minus_half = sb("minus_half", [P, 4])
    band = sb("band", [P, 8])
    band2 = sb("band2", [P, 2])
    wa = sb("wa", [P, CD, 3 * D])
    wp = sb("wp", [P, CD, D])
    wrt = sb("wrt", [P, CD, EXPERTS])
    bqk = sb("bqk", [P, 4])
    wah = sb("wah", [P, CD, 3 * D], F16)
    wal = sb("wal", [P, CD, 3 * D], F16)
    bv = sb("bv", [P, HEADS, DH])
    bp = sb("bp", [P, D])
    brt = sb("brt", [P, EXPERTS])
    lng = sb("lng", [P, CD])
    lnb = sb("lnb", [P, CD])
    bng = sb("bng", [P, CD])
    bnb = sb("bnb", [P, CD])
    bnm = sb("bnm", [P, CD])
    bnv = sb("bnv", [P, CD])
    bns = sb("bns", [P, CD])
    bnt = sb("bnt", [P, CD])
    qm = [sb(f"qm{q}", [P, JOBS, SEQ], F16) for q in range(2)]
    km = [sb(f"km{q}", [P, HEADS, SEQP], F16) for q in range(2)]
    ones = sb("ones", [P, 2, SEQP], F16)
    zero = sb("zero", [2, JOBS // 2, SEQ], F16)
    v = [sb(f"v{q}", [P, 3, HEADS, 2 * DH]) for q in range(2)]
    mx = [sb(f"mx{u}", [P, 3, P]) for u in range(2)]
    weights_in = sem("weights_in")
    pool_set = sem("pool_set")
    dve_set = sem("dve_set")
    setup_done = sem("setup_done")
    ones_placed = sem("ones_placed")
    return Constants(band, band2, bnb, bng, bnm, bns, bnt, bnv, bp, bqk, brt, bv, ident, ident16, km, later,
                     lnb, lng, minus_half, mx, ones, qm, v, wa, wah, wal, wp, wrt, zero, weights_in,
                     pool_set, dve_set, setup_done, ones_placed)


def load_constants(sp, c, w_attn, b_attn, w_proj, b_proj, ln_g, ln_b, bn_g, bn_b, bn_mean, bn_var, w_r, b_r):
    col = "(c p) -> p c"
    sp.dma_start(c.wa[:], w_attn.rearrange("(c p) n -> p c n", p=P)).then_inc(c.weights_in, 16)
    sp.dma_start(c.wp[:], w_proj.rearrange("(c p) n -> p c n", p=P)).then_inc(c.weights_in, 16)
    sp.dma_start(c.wrt[:], w_r.rearrange("(c p) n -> p c n", p=P)).then_inc(c.weights_in, 16)
    sp.dma_start(c.bqk[:], b_attn[0:2 * D].rearrange(col, p=P), allow_slow_non_contiguous=True).then_inc(c.weights_in, 16)
    sp.dma_start(c.bv[:].rearrange("p h d -> p (h d)"),
                 b_attn[2 * D:3 * D].unsqueeze(0).broadcast_to([P, D])).then_inc(c.weights_in, 16)
    sp.dma_start(c.bp[:], b_proj.unsqueeze(0).broadcast_to([P, D])).then_inc(c.weights_in, 16)
    sp.dma_start(c.brt[:], b_r.unsqueeze(0).broadcast_to([P, EXPERTS])).then_inc(c.weights_in, 16)
    for dst, src in ((c.lng, ln_g), (c.lnb, ln_b), (c.bng, bn_g), (c.bnb, bn_b), (c.bnm, bn_mean), (c.bnv, bn_var)):
        sp.dma_start(dst[:], src.rearrange(col, p=P), allow_slow_non_contiguous=True).then_inc(c.weights_in, 16)


def fill_constants(pool, c):
    for q in range(2):
        pool.memset(c.km[q][0:R3], 0.0).then_inc(c.ones_placed, 1)
    pool.memset(c.ident[:], 0.0).then_inc(c.pool_set, 1)
    pool.memset(c.ident16[:], 0.0).then_inc(c.pool_set, 1)
    pool.memset(c.later[:], 0.0).then_inc(c.pool_set, 1)
    pool.memset(c.minus_half[:], -0.5).then_inc(c.pool_set, 1)
    pool.memset(c.band[:], 1.0).then_inc(c.pool_set, 1)
    pool.wait_ge(c.pool_set, 5)
    pool.memset(c.ones[:], 1.0).then_inc(c.pool_set, 1)
    pool.wait_ge(c.pool_set, 6)
    for t in (c.ident, c.ident16):
        pool.affine_select(out=t[:], in_=t[:], compare_op=ALU.not_equal, fill=1.0, base=0,
                           pattern=[[-1, P]], channel_multiplier=1).then_inc(c.pool_set, 1)
    pool.affine_select(out=c.later[:], in_=c.later[:], compare_op=ALU.is_ge, fill=MASKED, base=0,
                       pattern=[[-1, P]], channel_multiplier=1).then_inc(c.pool_set, 1)
    pool.wait_ge(c.pool_set, 9)
    pool.affine_select(out=c.ones[R3:P], in_=c.ones[R3:P], compare_op=ALU.is_equal, fill=0.0, base=0,
                       pattern=[[-1, 2], [0, SEQP]], channel_multiplier=1).then_inc(c.pool_set, 1)
    pool.wait_ge(c.pool_set, 10)
    pool.affine_select(out=c.band[:], in_=c.band[:], compare_op=ALU.is_ge, fill=0.0, base=0,
                       pattern=[[-DH, 8]], channel_multiplier=1).then_inc(c.pool_set, 1)
    pool.wait_ge(c.pool_set, 11)
    pool.affine_select(out=c.band[:], in_=c.band[:], compare_op=ALU.is_ge, fill=0.0, base=DH - 1,
                       pattern=[[DH, 8]], channel_multiplier=-1).then_inc(c.pool_set, 1)
    pool.wait_ge(c.weights_in, 13 * 16)
    pool.tensor_scalar(c.bns[:], c.bnv[:], 1.0, EPS, ALU.mult, ALU.add).then_inc(c.pool_set, 1)
    pool.wait_ge(c.pool_set, 13)
    pool.tensor_tensor(c.bns[:], c.bns[:], c.minus_half[:, 0:CD], ALU.pow).then_inc(c.pool_set, 1)


def prepare_constants(dve, c):
    for q in range(2):
        dve.memset(c.qm[q][R3:P], 0.0)
        dve.memset(c.v[q][:], 0.0)
        dve.memset(c.mx[q][:], 0.0)
    dve.memset(c.zero[:], 0.0).then_inc(c.setup_done, 1)
    dve.wait_ge(c.setup_done, 1)
    for q in range(2):
        dve.memset(c.v[q][:, :, :, DH:DH + 1], 1.0)
    dve.wait_ge(c.weights_in, 13 * 16)
    dve.tensor_scalar(c.bqk[:, 0:2], c.bqk[:, 0:2], 0.25, None, ALU.mult)
    dve.tensor_scalar(c.wa[:, :, 0:D], c.wa[:, :, 0:D], 0.25, None, ALU.mult).then_inc(c.setup_done, 1)
    dve.wait_ge(c.setup_done, 2)
    dve.tensor_copy(c.wah[:], c.wa[:]).then_inc(c.setup_done, 1)
    dve.wait_ge(c.setup_done, 3)
    dve.tensor_tensor(c.wal[:], c.wa[:], c.wah[:], ALU.subtract).then_inc(c.dve_set, 1)
    dve.wait_ge(c.pool_set, NEED_POOL)
    for q in range(2):
        dve.tensor_copy(c.km[q][R3:P].rearrange("p (c r) k -> p c r k", r=2),
                        c.ones[R3:P].unsqueeze(1).broadcast_to([P - R3, JOBS, 2, SEQP])).then_inc(c.ones_placed, 1)
    dve.reduce_max(c.band2[:], c.band[:].rearrange("p (i r) -> p r i", r=2), AX.X)
    dve.tensor_tensor(c.bns[:], c.bns[:], c.bng[:], ALU.mult).then_inc(c.setup_done, 1)
    dve.wait_ge(c.setup_done, 4)
    dve.tensor_tensor(c.bnt[:], c.bns[:], c.bnm[:], ALU.mult).then_inc(c.setup_done, 1)
    dve.wait_ge(c.setup_done, 5)
    dve.tensor_tensor(c.bnt[:], c.bnb[:], c.bnt[:], ALU.subtract)
    dve.tensor_scalar(c.bns[:], c.bns[:], 1.0 / SEQ, None, ALU.mult).then_inc(c.setup_done, 1)
    dve.wait_ge(c.setup_done, 6)


def build_layer(nc, c, scratch, txt, w_down, b_down, w_up, b_up, out):
    ctx = ExitStack()
    with ctx:
        def sb(name, shape, dt=F32):
            return ctx.enter_context(nc.sbuf_tensor(name, shape, dt))

        def sem(name):
            return ctx.enter_context(nc.semaphore(name))

        band2, bns, bnt, bp, bqk, brt = c.band2, c.bns, c.bnt, c.bp, c.bqk, c.brt
        bv, ident, ident16, km, later, lnb = c.bv, c.ident, c.ident16, c.km, c.later, c.lnb
        lng, minus_half, mx, ones, qm, v = c.lng, c.minus_half, c.mx, c.ones, c.qm, c.v
        wah, wal, wp, wrt, zero = c.wah, c.wal, c.wp, c.wrt, c.zero
        h = sb("h", [P, 3, D])
        stats = sb("stats", [P, 3, 6])
        mv = sb("mv", [P, 3, 2])
        var1 = sb("var1", [P, 3])
        rstd1 = sb("rstd1", [P, 3])
        xn = sb("xn", [P, 3, D])
        xh = sb("xh", [P, CD, SEQ], F16)
        xl = sb("xl", [P, CD, SEQ], F16)
        qh = sb("qh", [P, CD, SEQ], F16)
        ql = sb("ql", [P, CD, SEQ], F16)
        kh = sb("kh", [P, CD, SEQ], F16)
        kl = sb("kl", [P, CD, SEQ], F16)
        kp = [sb(f"kpairs{q}", [R3, JOBS, SEQ], F16) for q in range(2)]
        pr = [sb(f"pr{s}", [P, 3, W0 + W2]) for s in range(PSLOTS)]
        ot = [sb(f"ot{q}", [P, 4, SEQ]) for q in range(2)]
        rden = sb("rden", [P, 3, HEADS])
        on = sb("on", [P, 3, D])
        ont = sb("ont", [P, CD, SEQ])
        res = sb("res", [P, 3, D])
        h2 = [sb(f"h2{q}", [P, 3, D]) for q in range(2)]
        stats2 = sb("stats2", [P, 3, 6])
        mv2 = sb("mv2", [P, 3, 2])
        var2 = sb("var2", [P, 3])
        rstd2 = sb("rstd2", [P, 3])
        zn = sb("zn", [P, 3, D])
        zt = sb("zt", [P, CD, SEQ])
        zsum = sb("zsum", [P, CD])
        zb = sb("zb", [P, CD])
        logit = sb("logit", [P, EXPERTS])
        top = sb("top", [P, 8])
        topi = sb("topi", [P, 8], U32)
        shifted = sb("shifted", [P, EXPERTS])
        expd = sb("expd", [P, EXPERTS])
        esum = sb("esum", [P, 1])
        gate = sb("gate", [P, 1])
        wd = sb("wd", [P, CD, HID])
        wu = sb("wu", [HID + 1, D])
        bd = sb("bd", [HID, 1])
        hid = sb("hid", [HID + 1, SEQ])
        ob = sb("ob", [P, 3, D])

        st = ctx.enter_context(nc.psum_tensor("st", [P, 3, 512], F32))
        sc = ctx.enter_context(nc.psum_tensor("sc", [P, 3, 512], F32))
        banks = [ctx.enter_context(nc.psum_tensor(f"shared{q}", [P, 512], F32)) for q in range(2)]
        bank_of = {n: banks[q] for n, _, q in SLICES}

        made = {n: sem(f"made_{n}") for n, _, _ in SLICES}
        taken = {n: sem(f"taken_{n}") for n, _, _ in SLICES}
        memory_set = sem("memory_set")
        h_in = sem("h_in")
        stats_ready = sem("stats_ready")
        mv_ready = sem("mv_ready")
        var_ready = sem("var_ready")
        rstd_ready = sem("rstd_ready")
        xn_ready = sem("xn_ready")
        xh_ready = sem("xh_ready")
        qh_ready = sem("qh_ready")
        kh_ready = sem("kh_ready")
        nm_part = sem("nm_part")
        q_placed = [sem(f"q_placed{c}") for c in range(CD)]
        k_placed = sem("k_placed")
        km_ready = sem("km_ready")
        sc_ready = sem("sc_ready")
        mx_ready = sem("mx_ready")
        st_ready = sem("st_ready")
        exp_done = sem("exp_done")
        causal = sem("causal")
        rden_ready = sem("rden_ready")
        res_in = sem("res_in")
        res_ready = sem("res_ready")
        stats2_ready = sem("stats2_ready")
        mv2_ready = sem("mv2_ready")
        var2_ready = sem("var2_ready")
        rstd2_ready = sem("rstd2_ready")
        zn_ready = sem("zn_ready")
        zb_mul = sem("zb_mul")
        zb_ready = sem("zb_ready")
        top_ready = sem("top_ready")
        topi_ready = sem("topi_ready")
        shifted_ready = sem("shifted_ready")
        esum_ready = sem("esum_ready")
        gate_ready = sem("gate_ready")
        expert_in = sem("expert_in")
        stored = sem("stored")
        passed = {n: sem(f"passed_{n}") for n in ("sp", "pool", "dve", "pe")}

        with nc.Block() as block:

            @block.sync
            def _(sp):
                sp.wait_ge(memory_set, 1)

                def load(dst, b, sm):
                    sp.dma_start(dst[:, 0:2, :], scratch[bass.ds(b.at, 1), :, :].rearrange("b (t p) l -> p (b t) l", p=P)).then_inc(sm, 16)
                    sp.dma_start(dst[0:TXT, 2:3, :], txt[bass.ds(b.at, 1), :, :].rearrange("b p l -> p b l")).then_inc(sm, 16)

                def place(dst, parts, chunks, placed):
                    for k, src in enumerate(parts):
                        for i in range(4):
                            sp.dma_start(dst[HR * k:HR * k + HR].rearrange("r (c i) k -> r c i k", c=CD)[:, chunks, i, :],
                                         src[HR * i:HR * i + HR, chunks, :]).then_inc(placed, 16)

                def place_q(b, c):
                    sp.wait_ge(taken[f"q{c}"], b.at + 1)
                    need(sp, st_ready, 2 * JOBS * (b.at - 1) - (JOBS if c == 0 else 0))
                    sp.sem_inc(passed["sp"], 1)
                    sp.dma_start(qm[b.par][R3:R3 + 2, 4 * c:4 * c + 4, :], zero[:]).then_inc(q_placed[c], 16)
                    place(qm[b.par], (qh, ql, qh), slice(c, c + 1), q_placed[c])

                def body(m, e):
                    b = batch(m, e)
                    if live(b):
                        need(sp, taken["pr2"], b.at)
                        sp.sem_inc(passed["sp"], 1)
                        load(res, b, res_in)
                    b = batch(m, e + 3)
                    if live(b):
                        need(sp, xn_ready, 3 * b.at)
                        sp.sem_inc(passed["sp"], 1)
                        load(h, b, h_in)
                    b = batch(m, e + 2)
                    if live(b):
                        place_q(b, 0)
                        sp.wait_ge(taken["k1"], b.at + 1)
                        sp.sem_inc(passed["sp"], 1)
                        place(kp[b.par], (kh, kh, kl), slice(0, CD), k_placed)
                    b = batch(m, e - 2)
                    if live(b):
                        sp.wait_ge(taken["fu2"], b.at + 1)
                        sp.sem_inc(passed["sp"], 1)
                        o = out[bass.ds(b.at, 1), :, :]
                        sp.dma_start(o[:, 0:HK, :].rearrange("b (t p) l -> p (b t) l", p=P), ob[:, 0:2, :]).then_inc(stored, 16)
                        sp.dma_start(o[:, HK:SEQ, :].rearrange("b p l -> p b l"), ob[0:TXT, 2:3, :]).then_inc(stored, 16)
                    b = batch(m, e - 1)
                    if live(b):
                        sp.wait_ge(topi_ready, b.at + 1)
                        sp.sem_inc(passed["sp"], 1)
                        x = sp.value_load(topi[0:1, 0:1], min_val=0, max_val=EXPERTS - 1)
                        one = bass.ds(x, 1)
                        sp.dma_start(wd[:], w_down[one, :, :].rearrange("e (c p) f -> p (e c) f", p=P)).then_inc(expert_in, 16)
                        sp.dma_start(bd[:], b_down[one, :].rearrange("e f -> f e"), allow_slow_non_contiguous=True).then_inc(expert_in, 16)
                        sp.dma_start(wu[0:HID, :], w_up[one, :, :].rearrange("e f d -> (e f) d")).then_inc(expert_in, 16)
                        sp.dma_start(wu[HID:HID + 1, :], b_up[one, :]).then_inc(expert_in, 16)
                    b = batch(m, e + 2)
                    if live(b):
                        place_q(b, 1)

                load(h, batch(0, 0), h_in)
                iterations(sp, body)
                sp.wait_ge(stored, 32 * BATCH)

            @block.gpsimd
            def _(pool):
                def power(src, scale, eps, var, rstd, b, got, mid, ready):
                    pool.wait_ge(got, 3 * b.at + 3)
                    pool.sem_inc(passed["pool"], 1)
                    pool.tensor_scalar(var[:], src[:, :, 1], scale, eps, ALU.mult, ALU.add).then_inc(mid, 1)
                    pool.wait_ge(mid, b.at + 1)
                    pool.sem_inc(passed["pool"], 1)
                    pool.tensor_tensor(rstd[:], var[:], minus_half[:, 0:3], ALU.pow).then_inc(ready, 1)

                def body(m, e):
                    now = batch(m, e)
                    for j in range(JOBS):
                        if live(now):
                            p = pr[j % PSLOTS]
                            pool.wait_ge(exp_done, 2 * (JOBS * now.at + j) + 2)
                            pool.sem_inc(passed["pool"], 1)
                            two = [[0, 2], [1, P]]
                            for ap, pat in ((p[:, 0:2, 0:P], two),
                                            (p[:, 2, :].rearrange("p (a c) -> p a c", c=W1)[:, :, 0:P], two),
                                            (p[:, 0:2, W0:W0 + W2], [[0, 2], [1, W2]])):
                                pool.affine_select(out=ap, in_=ap, compare_op=ALU.is_ge, fill=0.0, base=0,
                                                   pattern=pat, channel_multiplier=-1).then_inc(causal, 1)
                        b = batch(m, e - 1)
                        if j == WHEN["add bias"] and live(b):
                            pool.wait_ge(res_in, 32 * b.at + 32)
                            pool.sem_inc(passed["pool"], 1)
                            pool.tensor_tensor(res[:], res[:], bp[:].unsqueeze(1).broadcast_to([P, 3, D]), ALU.add).then_inc(res_ready, 1)
                        if j == WHEN["power 1"] and live(batch(m, e + 2)):
                            power(mv, 1.0, EPS, var1, rstd1, batch(m, e + 2), mv_ready, var_ready, rstd_ready)
                        if j == WHEN["power 2"] and live(b):
                            power(mv2, 1.0 + EPS, EPS * EPS, var2, rstd2, b, mv2_ready, var2_ready, rstd2_ready)

                iterations(pool, body)

            @block.scalar
            def _(act):
                act.wait_ge(memory_set, 1)

                def take(name, b):
                    db = bank_of[name]
                    act.wait_ge(made[name], b.at + 1)
                    if name in ("xt0", "xt1"):
                        act.copy(xh[:, int(name[2]), :], db[:, 0:SEQ]).then_inc(xh_ready, 1)
                    elif name in ("q0", "q1"):
                        c = int(name[1])
                        need(act, q_placed[c], Q_DMAS * b.at)
                        act.activation(qh[:, c, :], db[:, 0:SEQ], ACT.Identity, bias=bqk[:, c:c + 1]).then_inc(qh_ready, 1)
                    elif name in ("k0", "k1"):
                        c = int(name[1])
                        need(act, k_placed, K_DMAS * b.at)
                        act.activation(kh[:, c, :], db[:, 0:SEQ], ACT.Identity, bias=bqk[:, 2 + c:3 + c]).then_inc(kh_ready, 1)
                    elif name in ("nm0", "nm1"):
                        for i in range(4):
                            done = taken[name] if i == 3 else nm_part
                            act.mul(qm[b.par][R3:P, 4 * int(name[2]) + i, :], db[HR * i:HR * i + HR, 0:SEQ], -1.0).then_inc(done, 1)
                    elif name in ("ox0", "ox1"):
                        act.copy(ont[:, int(name[2]), :], db[:, 0:SEQ]).then_inc(taken[name], 1)
                    elif name in ("zt0", "zt1"):
                        c = int(name[2])
                        act.activation(zt[:, c, :], db[:, 0:SEQ], ACT.Identity, bias=lnb[:, c:c + 1], scale=lng[:, c:c + 1],
                                       accum_out=zsum[:, c:c + 1]).then_inc(taken[name], 1)
                    elif name == "rt":
                        act.wait_ge(shifted_ready, b.at + 1)
                        act.activation(expd[:], shifted[:], ACT.Exp, accum_out=esum[:]).then_inc(esum_ready, 1)
                    elif name == "fd":
                        act.activation(hid[0:HID, :], db[0:HID, 0:SEQ], ACT.Relu, bias=bd[:]).then_inc(taken[name], 1)
                    elif name[0:2] == "pv":
                        act.copy(ot[b.par][:, int(name[2]), :], db[:, 0:SEQ]).then_inc(taken[name], 1)

                def exps(b, j):
                    p = pr[j % PSLOTS]
                    act.wait_ge(st_ready, 2 * (JOBS * b.at + j) + 1)
                    need(act, made[f"pv{(j - 4) % JOBS // 2}"], b.at + (1 if j >= 4 else 0))
                    act.activation(p[:, 0:2, :], st[:, 0:2, 0:W0 + W2], ACT.Exp).then_inc(exp_done, 1)
                    act.wait_ge(st_ready, 2 * (JOBS * b.at + j) + 2)
                    act.activation(p[:, 2, :], st[:, 2, 0:2 * W1], ACT.Exp).then_inc(exp_done, 1)

                def body(m, e):
                    for j in range(JOBS):
                        for item in STEPS[j]:
                            if item == "st1" and live(batch(m, e)):
                                exps(batch(m, e), j)
                            elif not isinstance(item, str) and live(batch(m, e + item[1])):
                                if item[0] in ACT_TAKES:
                                    take(item[0], batch(m, e + item[1]))

                iterations(act, body)

            @block.vector
            def _(dve):
                dve.memset(hid[HID:HID + 1, :], 1.0)
                dve.memset(h[:, 2, :], 0.0)
                dve.memset(res[:, 2, :], 0.0)
                for q in range(2):
                    dve.memset(h2[q][:, 2, :], 0.0)
                dve.memset(on[:, 2, :], 0.0).then_inc(memory_set, 1)
                dve.wait_ge(memory_set, 1)

                def statistics(src, stat, mean_var, b, ready, done):
                    for t in range(3):
                        dve.bn_stats(stat[:, t, :], src[:, t, :]).then_inc(ready, 1)
                    dve.wait_ge(ready, 3 * b.at + 3)
                    dve.sem_inc(passed["dve"], 1)
                    for t in range(3):
                        dve.bn_aggr(mean_var[:, t, :], stat[:, t, :]).then_inc(done, 1)

                def normalise(dst, src, mean_var, rstd, b, got, done):
                    dve.wait_ge(got, b.at + 1)
                    dve.sem_inc(passed["dve"], 1)
                    for t in range(3):
                        dve.tensor_scalar(dst[:, t, :], src[:, t, :], mean_var[:, t, 0:1], rstd[:, t:t + 1],
                                          ALU.subtract, ALU.mult).then_inc(done, 1)

                def first_norm_stats(b):
                    dve.wait_ge(h_in, 32 * b.at + 32)
                    statistics(h, stats, mv, b, stats_ready, mv_ready)

                def take(name, b):
                    db = bank_of[name]
                    if name in ("xt0", "xt1"):
                        c = int(name[2])
                        dve.wait_ge(xh_ready, 2 * b.at + c + 1)
                        dve.tensor_tensor(xl[:, c, :], db[:, 0:SEQ], xh[:, c, :], ALU.subtract).then_inc(taken[name], 1)
                    elif name in ("q0", "q1"):
                        c = int(name[1])
                        dve.wait_ge(qh_ready, 2 * b.at + c + 1)
                        dve.scalar_tensor_tensor(ql[:, c, :], db[:, 0:SEQ], bqk[:, c:c + 1], qh[:, c, :],
                                                 ALU.add, ALU.subtract).then_inc(taken[name], 1)
                    elif name in ("k0", "k1"):
                        c = int(name[1])
                        dve.wait_ge(kh_ready, 2 * b.at + c + 1)
                        dve.scalar_tensor_tensor(kl[:, c, :], db[:, 0:SEQ], bqk[:, 2 + c:3 + c], kh[:, c, :],
                                                 ALU.add, ALU.subtract).then_inc(taken[name], 1)
                    elif name == "v01":
                        dve.wait_ge(made[name], b.at + 1)
                        dve.tensor_tensor(v[b.par][:, 0:2, :, 0:DH], db[:].rearrange("p (t h d) -> p t h d", t=2, d=DH),
                                          bv[:].unsqueeze(1).broadcast_to([P, 2, HEADS, DH]), ALU.add).then_inc(taken[name], 1)
                    elif name == "v2":
                        dve.wait_ge(made[name], b.at + 1)
                        dve.tensor_tensor(v[b.par][0:TXT, 2, :, 0:DH], db[0:TXT, 0:D].rearrange("p (h d) -> p h d", d=DH),
                                          bv[0:TXT], ALU.add).then_inc(taken[name], 1)
                    elif name in ("ot0", "ot1", "ot2"):
                        t = int(name[2])
                        n = TXT if t == 2 else P
                        o = db[0:n, :].rearrange("p (h d) -> p h d", d=2 * DH)
                        dve.wait_ge(made[name], b.at + 1)
                        dve.reciprocal(rden[0:n, t, :], o[:, :, DH]).then_inc(rden_ready, 1)
                        dve.wait_ge(rden_ready, 3 * b.at + t + 1)
                        dve.tensor_tensor(on[0:n, t, :].rearrange("p (h d) -> p h d", d=DH), o[:, :, 0:DH],
                                          rden[0:n, t, :].unsqueeze(2).broadcast_to([n, HEADS, DH]), ALU.mult).then_inc(taken[name], 1)
                    elif name == "pr01":
                        dve.wait_ge(res_ready, b.at + 1)
                        dve.wait_ge(made[name], b.at + 1)
                        dve.tensor_tensor(h2[b.par][:, 0:2, :], db[:].rearrange("p (t n) -> p t n", t=2), res[:, 0:2, :],
                                          ALU.add).then_inc(taken[name], 1)
                    elif name == "pr2":
                        dve.wait_ge(made[name], b.at + 1)
                        dve.tensor_tensor(h2[b.par][0:TXT, 2, :], db[0:TXT, 0:D], res[0:TXT, 2, :], ALU.add).then_inc(taken[name], 1)
                        dve.wait_ge(taken["pr01"], b.at + 1)
                        dve.wait_ge(taken["pr2"], b.at + 1)
                        statistics(h2[b.par], stats2, mv2, b, stats2_ready, mv2_ready)
                    elif name == "rt":
                        dve.wait_ge(made[name], b.at + 1)
                        dve.tensor_tensor(logit[:], db[:, 0:EXPERTS], brt[:], ALU.add).then_inc(taken[name], 1)
                        dve.wait_ge(taken[name], b.at + 1)
                        dve.sem_inc(passed["dve"], 1)
                        dve.max(top[:], logit[:]).then_inc(top_ready, 1)
                        dve.wait_ge(top_ready, b.at + 1)
                        dve.sem_inc(passed["dve"], 1)
                        dve.max_index(topi[:], top[:], logit[:]).then_inc(topi_ready, 1)
                        dve.tensor_scalar(shifted[:], logit[:], top[:, 0:1], None, ALU.subtract).then_inc(shifted_ready, 1)
                    elif name == "fu01":
                        dve.wait_ge(made[name], b.at + 1)
                        need(dve, stored, 32 * b.at)
                        dve.scalar_tensor_tensor(ob[:, 0:2, :], db[:].rearrange("p (t n) -> p t n", t=2), gate[:], h2[b.par][:, 0:2, :],
                                                 ALU.mult, ALU.add).then_inc(taken[name], 1)
                    elif name == "fu2":
                        dve.wait_ge(made[name], b.at + 1)
                        dve.scalar_tensor_tensor(ob[0:TXT, 2, :], db[0:TXT, 0:D], gate[0:TXT], h2[b.par][0:TXT, 2, :],
                                                 ALU.mult, ALU.add).then_inc(taken[name], 1)

                def keys_of_head(b, hd):
                    if hd == 0:
                        dve.wait_ge(k_placed, K_DMAS * b.at + K_DMAS)
                        dve.sem_inc(passed["dve"], 1)
                    dve.tensor_scalar(km[b.par][0:R3, hd, 0:SEQ], kp[b.par][:, hd // 2, :], band2[0:R3, hd % 2:hd % 2 + 1], None,
                                      ALU.mult).then_inc(km_ready, 1)

                def maxima(m, e, j):
                    b, jb = score_job(m, e, j)
                    if not live(b):
                        return
                    c = HR * (jb % 4)
                    rows = mx[jb // 4]
                    dve.wait_ge(sc_ready, 2 * (JOBS * b.at + jb) + 1)
                    dve.reduce_max(rows[:, 2, c:c + 2], sc[:, 0:2, 0:W0], AX.X).then_inc(mx_ready, 1)
                    dve.reduce_max(rows[0:TXT, 0, c:c + 2], sc[0:TXT, 0:2, W0:W0 + W2], AX.X).then_inc(mx_ready, 1)
                    dve.wait_ge(sc_ready, 2 * (JOBS * b.at + jb) + 2)
                    dve.reduce_max(rows[:, 1, c:c + 2], sc[:, 2, 0:2 * W1].rearrange("p (a c) -> p a c", a=2),
                                   AX.X).then_inc(mx_ready, 1)

                def body(m, e):
                    for j in range(JOBS):
                        for item in STEPS[j]:
                            if item == "sc":
                                b, pair = (batch(m, e + 1), j - 2) if j >= 2 else (batch(m, e), j + 6)
                                if live(b):
                                    keys_of_head(b, 2 * pair)
                                    keys_of_head(b, 2 * pair + 1)
                                maxima(m, e, j)
                            elif not isinstance(item, str) and live(batch(m, e + item[1])):
                                take(item[0], batch(m, e + item[1]))
                        b = batch(m, e - 2)
                        if j == 0 and live(b):
                            dve.wait_ge(esum_ready, b.at + 1)
                            dve.reciprocal(gate[:], esum[:]).then_inc(gate_ready, 1)
                        if j == 2 and live(b):
                            dve.wait_ge(gate_ready, b.at + 1)
                            dve.sem_inc(passed["dve"], 1)
                        b = batch(m, e + 2)
                        if j == WHEN["statistics"] and live(b):
                            first_norm_stats(b)
                        if j == WHEN["normalise 1"] and live(b):
                            normalise(xn, h, mv, rstd1, b, rstd_ready, xn_ready)
                        b = batch(m, e - 1)
                        if j == WHEN["normalise 2"] and live(b):
                            normalise(zn, h2[b.par], mv2, rstd2, b, rstd2_ready, zn_ready)
                        if j == WHEN["router input"] and live(b):
                            dve.wait_ge(taken["zt1"], b.at + 1)
                            dve.tensor_tensor(zb[:], zsum[:], bns[:], ALU.mult).then_inc(zb_mul, 1)
                            dve.wait_ge(zb_mul, b.at + 1)
                            dve.tensor_tensor(zb[:], zb[:], bnt[:], ALU.add).then_inc(zb_ready, 1)

                iterations(dve, body)

            @block.tensor
            def _(pe):
                pe.wait_ge(memory_set, 1)

                def tile(t):
                    return slice(P * t, min(P * t + P, SEQ))

                def make(name, b, before):
                    db = bank_of[name]
                    if before is not None:
                        pe.wait_ge(taken[before[0]], before[1].at + 1)
                    if name in ("xt0", "xt1"):
                        c = int(name[2])
                        pe.wait_ge(xn_ready, 3 * b.at + 3)
                        for t in range(3):
                            ins = pe.transpose(db[:, P * t:P * t + P], xn[:, t, P * c:P * c + P], ident[:])
                    elif name in ("q0", "q1", "k0", "k1"):
                        col = (D if name[0] == "k" else 0) + P * int(name[1])
                        pe.wait_ge(taken["xt1"], b.at + 1)
                        for c in range(CD):
                            for n, (w, x) in enumerate(((wah, xh), (wah, xl), (wal, xh))):
                                ins = pe.matmul(db[:, 0:SEQ], w[:, c, col:col + P], x[:, c, :],
                                                start=c + n == 0, stop=c * n == 2)
                    elif name in ("v01", "v2"):
                        for n, t in enumerate((0, 1) if name == "v01" else (2,)):
                            k = tile(t)
                            for c in range(CD):
                                for i, (x, w) in enumerate(((xh, wah), (xh, wal), (xl, wah))):
                                    ins = pe.matmul(db[0:k.stop - k.start, D * n:D * n + D], x[:, c, k], w[:, c, 2 * D:3 * D],
                                                    start=c + i == 0, stop=c * i == 2)
                    elif name in ("nm0", "nm1"):
                        u = int(name[2])
                        pe.wait_ge(mx_ready, 3 * (JOBS * b.at + 4 * u + 4))
                        for t, (q0, q1) in enumerate(QT):
                            n = q1 - q0
                            ins = pe.transpose(db[:, q0:q1], mx[u][0:n, t, :], ident[0:n, 0:n])
                    elif name in ("ot0", "ot1", "ot2"):
                        k = tile(int(name[2]))
                        pe.wait_ge(taken["pv3"], b.at + 1)
                        for g in range(4):
                            ins = pe.transpose(db[0:k.stop - k.start, P * g:P * g + P], ot[b.par][:, g, k], ident[:])
                    elif name in ("ox0", "ox1"):
                        c = int(name[2])
                        pe.wait_ge(taken["ot2"], b.at + 1)
                        for t in range(3):
                            k = tile(t)
                            n = k.stop - k.start
                            ins = pe.transpose(db[:, k], on[0:n, t, P * c:P * c + P], ident[0:n, 0:n])
                    elif name in ("pr01", "pr2"):
                        pe.wait_ge(taken["ox1"], b.at + 1)
                        for n, t in enumerate((0, 1) if name == "pr01" else (2,)):
                            k = tile(t)
                            for c in range(CD):
                                ins = pe.matmul(db[0:k.stop - k.start, D * n:D * n + D], ont[:, c, k], wp[:, c, :],
                                                start=c == 0, stop=c == CD - 1)
                    elif name in ("zt0", "zt1"):
                        c = int(name[2])
                        pe.wait_ge(zn_ready, 3 * b.at + 3)
                        for t in range(3):
                            k = tile(t)
                            n = k.stop - k.start
                            ins = pe.transpose(db[:, k], zn[0:n, t, P * c:P * c + P], ident[0:n, 0:n])
                    elif name == "rt":
                        pe.wait_ge(zb_ready, b.at + 1)
                        for c in range(CD):
                            ins = pe.matmul(db[:, 0:EXPERTS], zb[:, c:c + 1].broadcast_to([P, P]), wrt[:, c, :],
                                            start=c == 0, stop=c == CD - 1)
                    elif name == "fd":
                        pe.wait_ge(expert_in, 64 * b.at + 64)
                        pe.wait_ge(taken["zt1"], b.at + 1)
                        for c in range(CD):
                            ins = pe.matmul(db[0:HID, 0:SEQ], wd[:, c, :], zt[:, c, :], start=c == 0, stop=c == CD - 1)
                    elif name in ("fu01", "fu2"):
                        pe.wait_ge(taken["fd"], b.at + 1)
                        for n, t in enumerate((0, 1) if name == "fu01" else (2,)):
                            k = tile(t)
                            ins = pe.matmul(db[0:k.stop - k.start, D * n:D * n + D], hid[:, k], wu[:], start=True, stop=True)
                    elif name[0:2] == "pv":
                        g = int(name[2])
                        if g == 0:
                            pe.wait_ge(taken["v2"], b.at + 1)
                        pe.wait_ge(causal, 3 * (JOBS * b.at + 2 * g + 2))
                        pe.sem_inc(passed["pe"], 1)
                        for n, (_, q0) in enumerate(KT):
                            for a in range(4):
                                p = pr[(2 * g + a // 2) % PSLOTS]
                                aa = a % 2
                                src = (p[:, aa, 0:W0], p[:, 2, W1 * aa:W1 * aa + W1], p[:, aa, W0:W0 + W2])[n]
                                ins = pe.matmul(db[32 * a:32 * a + 32, q0:SEQ], v[b.par][:, n, 4 * g + a, :], src,
                                                start=n == 0, stop=n == 2)
                    ins.then_inc(made[name], 1)

                def scores_t(b, j, part):
                    if part == 0 and j % 4 == 0:
                        pe.wait_ge(taken[f"nm{j // 4}"], b.at + 1)
                    need(pe, exp_done, 2 * (JOBS * b.at + j) - 1 + part)
                    for a in range(2):
                        hd = 2 * j + a
                        own = ((0, st[:, a, 0:W0]), (2, st[:, a, W0:W0 + W2]))
                        both = ((1, st[:, 2, W1 * a:W1 * a + W1]),)
                        for t, o in (own, both)[part]:
                            k0, q0 = KT[t]
                            ins = pe.matmul(o, km[b.par][:, hd, k0:k0 + P], qm[b.par][:, j, q0:SEQ], start=True, stop=True)
                    ins.then_inc(st_ready, 1)

                def scores(b, j):
                    pe.wait_ge(km_ready, HEADS * b.at + 2 * j + 2)
                    if j % 4 == 0:
                        pe.wait_ge(q_placed[j // 4], Q_DMAS * b.at + Q_DMAS)
                    for part in range(2):
                        need(pe, mx_ready, 3 * (JOBS * b.at + j) - 1 + part)
                        for a in range(2):
                            hd = 2 * j + a
                            own = ((0, sc[0:TXT, a, W0:W0 + W2]), (2, sc[:, a, 0:W0]))
                            both = ((1, sc[:, 2, W1 * a:W1 * a + W1]),)
                            for t, o in (own, both)[part]:
                                q0, q1 = QT[t]
                                n = q1 - q0
                                pe.matmul(o[:, q0:q1], ident16[:, 0:n], later[:, 0:n], start=True, stop=False, skip_group_check=True)
                                ins = pe.matmul(o, qm[b.par][:, j, q0:q1], km[b.par][:, hd, 0:q1],
                                                start=False, stop=True, skip_group_check=True)
                        ins.then_inc(sc_ready, 1)

                def body(m, e):
                    now = batch(m, e)
                    for j in range(JOBS):
                        for item in STEPS[j]:
                            if item == "sc":
                                b, jb = score_job(m, e, j)
                                if live(b):
                                    scores(b, jb)
                            elif isinstance(item, str):
                                if live(now):
                                    scores_t(now, j, int(item[2]))
                            elif live(batch(m, e + item[1])):
                                make(item[0], batch(m, e + item[1]), slice_before(m, e, item[0]))

                iterations(pe, body)


_INS = ['x', 'txt', 'L0_tok_log_dt', 'L0_tok_inv_A_real', 'L0_tok_A_imag', 'L0_tok_B_ri', 'L0_attn_w_attn',
        'L0_attn_b_attn', 'L0_attn_w_proj', 'L0_attn_b_proj', 'L0_ffn_ln_g', 'L0_ffn_ln_b', 'L0_ffn_bn_g',
        'L0_ffn_bn_b', 'L0_ffn_bn_mean', 'L0_ffn_bn_var', 'L0_ffn_Wr', 'L0_ffn_br', 'L0_ffn_W_down',
        'L0_ffn_b_down', 'L0_ffn_W_up', 'L0_ffn_b_up']


def kernel(**inputs):
    import numpy as _np
    import concourse.bacc as _bacc
    from concourse import mybir as _mybir
    from concourse.bass_utils import run_bass_kernel_spmd as _run

    nc = _bacc.Bacc("TRN2", target_bir_lowering=False, num_devices=1)
    arrays, args = {}, []
    for name in _INS:
        a = _np.ascontiguousarray(inputs[name])
        arrays[f"in_{name}_dram"] = a
        args.append(nc.dram_tensor(f"in_{name}_dram", a.shape, _mybir.dt.from_np(a.dtype), kind="ExternalInput").ap())
    out = nc.dram_tensor("out_0_dram", (32, 333, 256), _mybir.dt.float32, kind="ExternalOutput").ap()
    scratch = nc.dram_tensor("token_scratch", (32, 256, 256), _mybir.dt.float32, kind="Internal").ap()
    x, txt, log_dt, inv_a, a_imag, b_ri = args[:6]
    with ExitStack() as ctx:
        c = layer_constants(nc, ctx)
        build_tokens(nc, x, log_dt, inv_a, a_imag, b_ri, scratch, c, args[6:18])
        build_layer(nc, c, scratch, txt, *args[18:], out)
    r = _run(nc, [arrays], core_ids=[0])
    return r.results[0]["out_0_dram"]
```
